# Optimizing a Trainium2 kernel written in Bass

```python
import numpy as np
import jax
import jax.numpy as jnp

def _softmax(x, axis=-1):
    return jax.nn.softmax(x, axis=axis)

def _gelu(x):
    return jax.nn.gelu(x, approximate=True)

def _silu(x):
    return jax.nn.silu(x)

def _sigmoid(x):
    return jax.nn.sigmoid(x)

def _layernorm(x, axis=-1, eps=1e-05):
    m = jnp.mean(x, axis=axis, keepdims=True)
    v = jnp.var(x, axis=axis, keepdims=True)
    return (x - m) / jnp.sqrt(v + eps)

def _scatter_add(tgt, idx, src, axis=0):
    return tgt.at[idx].add(src)

def _segment_sum(src, seg, n):
    return jax.ops.segment_sum(src, seg, n)
kernel_name = 'mk_gnn_preln_d1_gnn_r64_d26a28'

def setup_inputs(seed: int=0):
    np.random.seed(seed)
    _w = jnp.asarray

    def _rec_inputs():
        import jax
        import jax.numpy as jnp
        _gk = jax.random.key(seed)
        x = -0.0001006 + 1 * jax.random.normal(jax.random.fold_in(_gk, 1), (100000, 96), jnp.float32)
        _s = jax.random.randint(jax.random.fold_in(_gk, 2), (25000,), 0, 100000, jnp.int32)
        _d = jax.random.randint(jax.random.fold_in(_gk, 3), (25000,), 0, 100000, jnp.int32)
        _loop = jnp.arange(100000, dtype=jnp.int32)
        src = jnp.concatenate([_s, _d, _loop])
        dst = jnp.concatenate([_d, _s, _loop])
        _o = jnp.argsort(dst, stable=True)
        src = src[_o]
        dst = dst[_o]
        return (x, src, dst)
    x, src, dst = _rec_inputs()

    def _L0_gnn_setup():
        import jax, jax.numpy as jnp
        import numpy as np
        N_NODES = 50000
        N_EDGES = 12500
        D_IN = 96
        D_OUT = 96
        key = jax.random.key(seed)
        k1, k2, k3, k4 = jax.random.split(key, 4)
        x = jax.random.normal(k1, (N_NODES, D_IN), dtype=jnp.float32)
        edge_index = jax.random.randint(k2, (2, N_EDGES), 0, N_NODES, dtype=jnp.int64)
        W = jax.random.normal(k3, (D_IN, D_OUT), dtype=jnp.float32) * (1.0 / np.sqrt(D_IN))
        b = jax.random.normal(k4, (D_OUT,), dtype=jnp.float32) * 0.01
        return {'x': x, 'edge_index': edge_index, 'W': W, 'b': b}
    _L0_gnn_all = _L0_gnn_setup()
    _L0_gnn_in = {k: v for k, v in _L0_gnn_all.items() if k in ('W', 'b')}
    del _L0_gnn_all
    return {'x': x, 'src': src, 'dst': dst, 'L0_gnn_W': _L0_gnn_in['W'], 'L0_gnn_b': _L0_gnn_in['b']}

def reference(x, src, dst, L0_gnn_W, L0_gnn_b):
    import jax
    import jax.numpy as jnp

    def _L0_gnn_ref(x, edge_index, W, b):
        import jax, jax.numpy as jnp
        import numpy as np
        N_NODES = 50000
        N_EDGES = 12500
        D_IN = 96
        D_OUT = 96
        num_nodes = x.shape[0]
        src, dst = (edge_index[0], edge_index[1])
        messages = x[src] @ W + b
        out = jax.ops.segment_sum(messages, dst, num_segments=num_nodes)
        deg = jax.ops.segment_sum(jnp.ones((dst.shape[0],), dtype=x.dtype), dst, num_segments=num_nodes)
        deg = jnp.clip(deg, 1.0, None)
        return out / deg[:, None]
    edge_index = jnp.stack([src, dst])
    h = jnp.maximum(_layernorm(x, axis=-1), 0.0)
    x = x + _L0_gnn_ref(h, edge_index, L0_gnn_W, L0_gnn_b)
    return x

_drawn_inputs = setup_inputs


def setup_inputs(seed=0):
    import zlib

    import numpy as np

    out = dict(_drawn_inputs(seed))
    spreads = {}
    factors = {'L0_gnn_b': 7.199}
    for name, (base, spread) in spreads.items():
        noise = np.random.default_rng([zlib.crc32(name.encode()), seed]).standard_normal(out[name].shape)
        drawn = base * np.exp(spread * noise) if base else spread * noise
        out[name] = jnp.asarray(drawn.astype(out[name].dtype))
    for name, factor in factors.items():
        out[name] = (out[name] * factor).astype(out[name].dtype)
    return out
```

```python
from contextlib import ExitStack

import concourse.bass as bass
from concourse import mybir

ALU = mybir.AluOpType
ACT = mybir.ActivationFunctionType
F32 = mybir.dt.float32
I32 = mybir.dt.int32

P = 128
EPS = 1e-5
EDGE_ROWS = 120
NODE_ROWS = 125


def gnn_layer(nc, x, src, dst, W, b, out):
    N, D = x.shape
    E = src.shape[0]
    A = D + 1
    EDGE_TILES = E // EDGE_ROWS
    NODE_TILES = N // NODE_ROWS
    assert EDGE_TILES * EDGE_ROWS == E and NODE_TILES * NODE_ROWS == N

    with ExitStack() as ctx:
        def sb(name, shape, dt=F32):
            return ctx.enter_context(nc.sbuf_tensor(name, shape, dt))

        def sem(name):
            return ctx.enter_context(nc.semaphore(name))

        acc_dram = nc.dram_tensor("acc_dram", [N + P, A], F32).ap()

        src_all = sb("src_all", [EDGE_ROWS, EDGE_TILES], I32)
        dst_all = sb("dst_all", [EDGE_ROWS, EDGE_TILES], I32)
        zeros = sb("zeros", [P, 8 * A])
        ident = sb("ident", [P, P])
        later = sb("later", [P, P])
        dump_row = sb("dump_row", [P, 1])
        Waug = sb("Waug", [A, A])
        gi_src = sb("gi_src", [EDGE_ROWS, 1], I32)
        gi_dst = sb("gi_dst", [EDGE_ROWS, 1], I32)
        gi_put = sb("gi_put", [EDGE_ROWS, 1], I32)
        g_dst = sb("g_dst", [EDGE_ROWS, 1])
        g_dstb = sb("g_dstb", [EDGE_ROWS, EDGE_ROWS])
        g_eq = sb("g_eq", [EDGE_ROWS, EDGE_ROWS])
        g_eql = sb("g_eql", [EDGE_ROWS, EDGE_ROWS])
        g_small = sb("g_small", [EDGE_ROWS, 16])
        g_x = sb("g_x", [EDGE_ROWS, D])
        g_acc = sb("g_acc", [EDGE_ROWS, A])
        g_h = sb("g_h", [EDGE_ROWS, A])
        g_new = sb("g_new", [EDGE_ROWS, A])
        n_acc = sb("n_acc", [NODE_ROWS, A])
        n_x = sb("n_x", [NODE_ROWS, D])
        n_zT = sb("n_zT", [A, NODE_ROWS])
        n_deg = sb("n_deg", [NODE_ROWS, 2])
        n_out = sb("n_out", [NODE_ROWS, D])
        ps = ctx.enter_context(nc.psum_tensor("ps", [P, 4, 512], F32))

        loaded = sem("loaded")
        zeroed = sem("zeroed")
        consts = sem("consts")
        dconsts = sem("dconsts")
        cleared = sem("cleared")
        g_chain = sem("g_chain")
        g_idx = sem("g_idx")
        g_gx = sem("g_gx")
        g_gacc = sem("g_gacc")
        g_dstT = sem("g_dstT")
        g_eqs = sem("g_eqs")
        g_var = sem("g_var")
        g_std = sem("g_std")
        g_scale = sem("g_scale")
        g_hs = sem("g_hs")
        g_sum = sem("g_sum")
        g_news = sem("g_news")
        g_put = sem("g_put")
        n_in = sem("n_in")
        n_T = sem("n_T")
        n_zTs = sem("n_zTs")
        n_mm = sem("n_mm")
        n_chain = sem("n_chain")
        n_done = sem("n_done")
        n_stored = sem("n_stored")
        pool_gate = sem("pool_gate")
        sp_gate = sem("sp_gate")
        dve_gate = sem("dve_gate")

        block = ctx.enter_context(nc.Block())

        @block.sync
        def _(sp):
            sp.dma_start(src_all[:, :], src.rearrange("(p t) -> p t", p=EDGE_ROWS)).then_inc(loaded, 16)
            sp.dma_start(dst_all[:, :], dst.rearrange("(p t) -> p t", p=EDGE_ROWS)).then_inc(loaded, 16)
            sp.dma_start(Waug[0:D, 0:D], W).then_inc(loaded, 16)
            sp.dma_start(Waug[D:A, 0:D], b.rearrange("(o d) -> o d", o=1)).then_inc(loaded, 16)
            sp.wait_ge(zeroed, 1)
            with sp.Fori(0, 100) as i:
                sp.dma_start(acc_dram[bass.ds(i * 1000, 1000), :].rearrange("(p r) a -> p (r a)", p=125),
                             zeros[0:125, :]).then_inc(cleared, 16)
            sp.dma_start(acc_dram[N:N + P, :], zeros[:, 0:A]).then_inc(cleared, 16)
            sp.wait_ge(g_put, 16 * EDGE_TILES)
            with sp.Fori(0, NODE_TILES) as i:
                sp.dma_start(n_acc[:, :], acc_dram[bass.ds(i * NODE_ROWS, NODE_ROWS), :]).then_inc(n_in, 16)
                sp.dma_start(n_x[:, :], x[bass.ds(i * NODE_ROWS, NODE_ROWS), :]).then_inc(n_in, 16)
                sp.wait_ge(n_done, i + 1)
                sp.dma_start(out[bass.ds(i * NODE_ROWS, NODE_ROWS), :], n_out[:, :]).then_inc(n_stored, 16)
                sp.wait_ge(n_stored, i * 16 + 16)
                sp.sem_inc(sp_gate, 1)

        @block.gpsimd
        def _(pool):
            pool.memset(ident[:, :], 0.0).then_inc(consts, 1)
            pool.memset(later[:, :], 1.0).then_inc(consts, 1)
            pool.iota(dump_row[:, :], [[0, 1]], base=N, channel_multiplier=1,
                      allow_small_or_imprecise_dtypes=True).then_inc(consts, 1)
            pool.wait_ge(consts, 3)
            pool.affine_select(out=ident[:, :], in_=ident[:, :], compare_op=ALU.not_equal, fill=1.0,
                               base=0, pattern=[[-1, P]], channel_multiplier=1).then_inc(consts, 1)
            pool.affine_select(out=later[:, :], in_=later[:, :], compare_op=ALU.is_gt, fill=0.0,
                               base=0, pattern=[[1, P]], channel_multiplier=-1).then_inc(consts, 1)
            pool.wait_ge(cleared, 16 * 101)
            with pool.Fori(0, EDGE_TILES) as i:
                pool.wait_ge(g_idx, i + 1)
                pool.sem_inc(pool_gate, 1)
                pool.indirect_dma_start(out=g_x[:, :], out_offset=None, in_=x,
                                        in_offset=bass.IndirectOffsetOnAxis(ap=gi_src[:, 0:1], axis=0)
                                        ).then_inc(g_gx, 16)
                pool.indirect_dma_start(out=g_acc[:, :], out_offset=None, in_=acc_dram,
                                        in_offset=bass.IndirectOffsetOnAxis(ap=gi_dst[:, 0:1], axis=0)
                                        ).then_inc(g_gacc, 16)
                pool.wait_ge(g_news, i + 1)
                pool.sem_inc(pool_gate, 1)
                pool.indirect_dma_start(out=acc_dram,
                                        out_offset=bass.IndirectOffsetOnAxis(ap=gi_put[:, 0:1], axis=0),
                                        in_=g_new[:, :], in_offset=None).then_inc(g_put, 16)
                pool.wait_ge(g_put, i * 16 + 16)

        @block.vector
        def _(dve):
            dve.memset(zeros[:, :], 0.0).then_inc(zeroed, 1)
            dve.memset(g_h[:, D:A], 1.0).then_inc(dconsts, 1)
            dve.memset(Waug[:, D:A], 0.0).then_inc(g_chain, 1)
            dve.wait_ge(g_chain, 1)
            dve.memset(Waug[D:A, D:A], 1.0).then_inc(dconsts, 1)
            dve.wait_ge(loaded, 64)
            dve.wait_ge(consts, 5)
            dve.wait_ge(dconsts, 2)
            C = 9
            with dve.Fori(0, EDGE_TILES) as i:
                c = i * C + 1
                dve.tensor_copy(gi_src[:, :], src_all[:, bass.ds(i, 1)]).then_inc(g_chain, 1)
                dve.tensor_copy(gi_dst[:, :], dst_all[:, bass.ds(i, 1)]).then_inc(g_chain, 1)
                dve.tensor_copy(g_dst[:, :], dst_all[:, bass.ds(i, 1)]).then_inc(g_chain, 1)
                dve.wait_ge(g_chain, c + 3)
                dve.tensor_copy(g_dstb[:, :], g_dst[:, 0:1].to_broadcast([EDGE_ROWS, EDGE_ROWS])).then_inc(g_idx, 1)
                dve.wait_ge(g_dstT, i + 1)
                dve.tensor_scalar(g_eq[:, :], ps[0:EDGE_ROWS, 0, 0:EDGE_ROWS], g_dst[:, 0:1], None,
                                  ALU.is_equal).then_inc(g_eqs, 1)
                dve.wait_ge(g_eqs, i + 1)
                dve.tensor_tensor_reduce(out=g_eql[:, :], in0=g_eq[:, :], in1=later[0:EDGE_ROWS, 0:EDGE_ROWS],
                                         scale=1.0, scalar=0.0, op0=ALU.mult, op1=ALU.add,
                                         accum_out=g_small[:, 8:9]).then_inc(g_chain, 1)
                dve.wait_ge(g_chain, c + 4)
                dve.tensor_scalar(g_small[:, 9:10], g_small[:, 8:9], 1.0, None, ALU.min).then_inc(g_chain, 1)
                dve.tensor_tensor(g_small[:, 10:11], dump_row[0:EDGE_ROWS, :], g_dst[:, 0:1],
                                  ALU.subtract).then_inc(g_chain, 1)
                dve.wait_ge(g_chain, c + 6)
                dve.scalar_tensor_tensor(out=gi_put[:, :], in0=g_small[:, 10:11], scalar=g_small[:, 9:10],
                                         in1=g_dst[:, :], op0=ALU.mult, op1=ALU.add).then_inc(g_chain, 1)
                dve.wait_ge(g_gx, i * 16 + 16)
                dve.bn_stats(g_small[:, 0:6], g_x[:, :]).then_inc(g_chain, 1)
                dve.wait_ge(g_chain, c + 8)
                dve.sem_inc(dve_gate, 1)
                dve.bn_aggr(g_small[:, 11:13], g_small[:, 0:6]).then_inc(g_chain, 1)
                dve.wait_ge(g_chain, c + 9)
                dve.tensor_scalar(g_small[:, 13:14], g_small[:, 12:13], EPS, None, ALU.add).then_inc(g_var, 1)
                dve.wait_ge(g_std, i + 1)
                dve.reciprocal(g_small[:, 15:16], g_small[:, 14:15]).then_inc(g_scale, 1)
                dve.wait_ge(g_scale, i * 2 + 1)
                dve.scalar_tensor_tensor(out=g_small[:, 8:9], in0=g_small[:, 11:12], scalar=-1.0,
                                         in1=g_small[:, 15:16], op0=ALU.mult, op1=ALU.mult).then_inc(g_scale, 1)
                dve.wait_ge(g_sum, i + 1)
                dve.wait_ge(g_gacc, i * 16 + 16)
                dve.tensor_tensor(g_new[:, :], ps[0:EDGE_ROWS, 1, 0:A], g_acc[:, :], ALU.add).then_inc(g_news, 1)
                dve.wait_ge(g_put, i * 16 + 16)
            with dve.Fori(0, NODE_TILES) as i:
                dve.wait_ge(n_T, i + 1)
                dve.tensor_copy(n_zT[:, :], ps[0:A, 2, 0:NODE_ROWS]).then_inc(n_zTs, 1)
                dve.wait_ge(n_mm, i + 1)
                dve.tensor_scalar(n_deg[:, 0:1], ps[0:NODE_ROWS, 3, D:A], 1.0, None, ALU.max).then_inc(n_chain, 1)
                dve.wait_ge(n_chain, i * 2 + 1)
                dve.reciprocal(n_deg[:, 1:2], n_deg[:, 0:1]).then_inc(n_chain, 1)
                dve.wait_ge(n_chain, i * 2 + 2)
                dve.scalar_tensor_tensor(out=n_out[:, :], in0=ps[0:NODE_ROWS, 3, 0:D], scalar=n_deg[:, 1:2],
                                         in1=n_x[:, :], op0=ALU.mult, op1=ALU.add).then_inc(n_done, 1)

        @block.scalar
        def _(act):
            act.wait_ge(consts, 5)
            act.wait_ge(dconsts, 2)
            with act.Fori(0, EDGE_TILES) as i:
                act.wait_ge(g_var, i + 1)
                act.activation(g_small[:, 14:15], g_small[:, 13:14], ACT.Sqrt).then_inc(g_std, 1)
                act.wait_ge(g_scale, i * 2 + 2)
                act.activation(g_h[:, 0:D], g_x[:, :], ACT.Relu, bias=g_small[:, 8:9],
                               scale=g_small[:, 15:16]).then_inc(g_hs, 1)

        @block.tensor
        def _(pe):
            pe.wait_ge(consts, 5)
            pe.wait_ge(dconsts, 2)
            with pe.Fori(0, EDGE_TILES) as i:
                pe.wait_ge(g_idx, i + 1)
                pe.transpose(ps[0:EDGE_ROWS, 0, 0:EDGE_ROWS], g_dstb[:, :],
                             ident[0:EDGE_ROWS, 0:EDGE_ROWS]).then_inc(g_dstT, 1)
                pe.wait_ge(g_eqs, i + 1)
                pe.wait_ge(g_hs, i + 1)
                pe.matmul(ps[0:EDGE_ROWS, 1, 0:A], g_eq[:, :], g_h[:, :], start=True, stop=True).then_inc(g_sum, 1)
            with pe.Fori(0, NODE_TILES) as i:
                pe.wait_ge(n_in, i * 32 + 32)
                pe.transpose(ps[0:A, 2, 0:NODE_ROWS], n_acc[:, :],
                             ident[0:NODE_ROWS, 0:NODE_ROWS]).then_inc(n_T, 1)
                pe.wait_ge(n_zTs, i + 1)
                pe.matmul(ps[0:NODE_ROWS, 3, 0:A], n_zT[:, :], Waug[:, :], start=True, stop=True).then_inc(n_mm, 1)


_INS = ["x", "src", "dst", "L0_gnn_W", "L0_gnn_b"]


def kernel(**inputs):
    import numpy as _np
    import concourse.bacc as _bacc
    from concourse import mybir as _mybir
    from concourse.bass_utils import run_bass_kernel_spmd as _run

    nc = _bacc.Bacc("TRN2", target_bir_lowering=False, num_devices=1)
    arrays, args = {}, []
    for name in _INS:
        a = _np.ascontiguousarray(inputs[name])
        arrays[f"in_{name}_dram"] = a
        args.append(nc.dram_tensor(f"in_{name}_dram", a.shape, _mybir.dt.from_np(a.dtype), kind="ExternalInput").ap())
    args.append(nc.dram_tensor("out_0_dram", inputs["x"].shape, _mybir.dt.float32, kind="ExternalOutput").ap())
    gnn_layer(nc, *args)
    r = _run(nc, [arrays], core_ids=[0])
    return r.results[0]["out_0_dram"]
```

```python
from contextlib import ExitStack

import concourse.bass as bass
from concourse import mybir

ALU = mybir.AluOpType
ACT = mybir.ActivationFunctionType
AX = mybir.AxisListType
F32 = mybir.dt.float32
I32 = mybir.dt.int32

P = 128
EPS = 1e-5
KEEP = mybir.dt.float32

SEG_ROWS = 125
SEGS = 12
SEG = 100
CAP = 56
ROUNDS = CAP // 8
SPREAD = 3
SRC_BITS = 17

TILES = 3
WINDOW = TILES * P
SLOTS = 2
GROUP = 4
SKIP = 56
RING = 3
TABLE_ROWS = 88

EDGE_ROWS = 120
NODE_ROWS = 125


def gnn_layer(nc, x, src, dst, W, b, out):
    N, D = x.shape
    E = src.shape[0]
    A = D + 1
    FAR = E - N
    assert SEG_ROWS * SEGS * SEG == E and N < 1 << SRC_BITS and SEG << SRC_BITS < 1 << 24

    STEP = GROUP * WINDOW
    STEPS = -(-N // STEP)
    BACK = STEPS * STEP - N
    WINDOWS = STEPS * GROUP
    BLOCKS = WINDOWS // TABLE_ROWS
    BLOCK_STEPS = TABLE_ROWS // GROUP
    assert BLOCKS * TABLE_ROWS == WINDOWS and STEPS % RING == 0
    PACKED = SLOTS * P
    LIST_ROWS = 126 * 400
    assert LIST_ROWS >= FAR + PACKED + 1
    GT = GROUP * TILES
    GS = GROUP * SLOTS
    LN = GT + GS
    LATE = P - SKIP

    EDGE_TILES = E // EDGE_ROWS
    NODE_TILES = N // NODE_ROWS
    assert EDGE_TILES * EDGE_ROWS == E and NODE_TILES * NODE_ROWS == N

    with ExitStack() as ctx:
        def sb(name, shape, dt=F32):
            return ctx.enter_context(nc.sbuf_tensor(name, shape, dt))

        def sem(name):
            return ctx.enter_context(nc.semaphore(name))

        ps = ctx.enter_context(nc.psum_tensor("ps", [P, 8, 512], F32))

        ident = sb("ident", [P, P])
        later = sb("later", [P, P])
        node_no = sb("node_no", [P, TILES, P])
        Waug = sb("Waug", [A, A])
        ones = sb("ones", [P, P])
        eps = sb("eps", [P, 1])
        dump_row = sb("dump_row", [P, 1])
        zeros = sb("zeros", [P, 800])
        c_pool = sem("c_pool")
        c_dve = sem("c_dve")
        w_loaded = sem("w_loaded")

        x_in = sb("x_in", [P, RING, GROUP, TILES * D])
        x_far = sb("x_far", [P, RING, GS, D])
        far_i = sb("far_i", [P, RING, GS], I32)
        far_n = sb("far_n", [P, RING, GS])
        stats = sb("stats", [P, RING, LN, 6])
        ln = sb("ln", [P, RING, 8, LN])
        h = sb("h", [P, RING, LN, A])
        hit0 = sb("hit0", [P, RING, GROUP, TILES, P])
        hit1 = sb("hit1", [P, RING, GROUP, TILES, LATE])
        zT = sb("zT", [A, GROUP, WINDOW])
        recip = sb("recip", [P, 2, GROUP // 2, TILES])
        scaled = sb("scaled", [P, 2, GROUP // 2, TILES, D])
        y = sb("y", [P, RING, GROUP, TILES * D])

        x_loaded = [sem(f"x_loaded{i}") for i in range(RING)]
        stored = [sem(f"stored{i}") for i in range(RING)]
        gathered = [sem(f"gathered{i}") for i in range(RING)]
        idx_ready = sem("idx_ready")
        s_chain = sem("s_chain")
        var_ready = sem("var_ready")
        std_ready = sem("std_ready")
        ln_ready = sem("ln_ready")
        hits_ready = sem("hits_ready")
        h_ready = sem("h_ready")
        z_ready = sem("z_ready")
        zT_ready = sem("zT_ready")
        m_ready = sem("m_ready")
        f_chain = sem("f_chain")
        f_read = sem("f_read")
        y_ready = sem("y_ready")
        all_stored = sem("all_stored")

        table = sb("table", [P, STEPS + RING, 2, GS])
        flag = sb("flag", [P, 4])
        flag_i = sb("flag_i", [1, 1], I32)

        early = ExitStack()

        def early_sb(name, shape, dt=F32):
            return early.enter_context(nc.sbuf_tensor(name, shape, dt))

        packed = [nc.dram_tensor(f"packed{i}", [LIST_ROWS, 2], F32).ap() for i in range(SPREAD)]
        e_src = early_sb("e_src", [SEG_ROWS, SEGS * SEG], I32)
        e_dst = early_sb("e_dst", [SEG_ROWS, SEGS * SEG], I32)
        e_next = early_sb("e_next", [SEG_ROWS, 3], I32)
        key = early_sb("key", [SEG_ROWS, SEGS, SEG])
        far = early_sb("far", [SEG_ROWS, SEGS * SEG])
        same = early_sb("same", [SEG_ROWS, SEGS * SEG])
        rev_pos = early_sb("rev_pos", [SEG_ROWS, SEGS * SEG])
        found = early_sb("found", [SEG_ROWS, SEGS, CAP])
        found_i = early_sb("found_i", [SEG_ROWS, SEGS, CAP], I32)
        part_i = early_sb("part_i", [SEG_ROWS, 2, SEGS, CAP], I32)
        valid = early_sb("valid", [SEG_ROWS, SEGS, CAP])
        slot_no = early_sb("slot_no", [SEG_ROWS, SEGS, CAP])
        tgt = early_sb("tgt", [SEG_ROWS, SEGS, CAP])
        pairs = early_sb("pairs", [SEG_ROWS, SEGS, CAP, 2])
        heads = early_sb("heads", [SEG_ROWS, SEGS + 3])
        head_no = early_sb("head_no", [SEG_ROWS, SEGS + 3])
        rank = early_sb("rank", [SEG_ROWS, SEGS + 3])
        rank_i = early_sb("rank_i", [SEG_ROWS, SEGS], I32)
        own_rows = early_sb("own_rows", [SEG_ROWS, SEGS])
        fine = early_sb("fine", [SEG_ROWS, 3])
        gap = early_sb("gap", [SEG_ROWS, 2, SEGS])
        faults = early_sb("faults", [P, 10])
        head_diag = early_sb("head_diag", [SEG_ROWS, SEG_ROWS, SEGS])
        below = early_sb("below", [TABLE_ROWS, SEG_ROWS * SEGS])
        below_c = early_sb("below_c", [TABLE_ROWS, BLOCKS, SEG])
        base = early_sb("base", [TABLE_ROWS, BLOCKS])
        late = early_sb("late", [TABLE_ROWS, BLOCKS])
        chunk = early_sb("chunk", [TABLE_ROWS, BLOCKS])
        chunk_i = early_sb("chunk_i", [TABLE_ROWS, BLOCKS], I32)
        chunk_dst = early_sb("chunk_dst", [TABLE_ROWS, BLOCKS, SEG], I32)
        start = early_sb("start", [TABLE_ROWS, BLOCKS])
        start_i = early_sb("start_i", [TABLE_ROWS, BLOCKS], I32)
        wpairs = early_sb("wpairs", [TABLE_ROWS, BLOCKS, SPREAD, (PACKED + 1) * 2])
        wedge = early_sb("wedge", [TABLE_ROWS, BLOCKS, 2, PACKED + 1])
        wtest = early_sb("wtest", [TABLE_ROWS, BLOCKS, 4])

        dst_loaded = sem("dst_loaded")
        src_loaded = sem("src_loaded")
        next_set = sem("next_set")
        next_loaded = sem("next_loaded")
        cleared = [sem(f"cleared{i}") for i in range(SPREAD)]
        rank_ready = sem("rank_ready")
        tests_ready = sem("tests_ready")
        tests_summed = sem("tests_summed")
        pairs_ready = sem("pairs_ready")
        scattered = sem("scattered")
        diag_ready = sem("diag_ready")
        heads_spread = sem("heads_spread")
        chunk_ready = sem("chunk_ready")
        chunk_loaded = sem("chunk_loaded")
        start_ready = sem("start_ready")
        wpairs_loaded = [sem(f"wpairs_loaded{i}") for i in range(BLOCKS)]
        wedge_ready = sem("wedge_ready")
        turned = sem("turned")
        turned_used = sem("turned_used")
        faults_ready = sem("faults_ready")
        faults_summed = sem("faults_summed")
        flag_ready = sem("flag_ready")
        d_chain = sem("d_chain")
        p_chain = sem("p_chain")

        early.close()
        acc_dram = nc.dram_tensor("acc_dram", [N + P, A], F32).ap()
        src_all = sb("src_all", [EDGE_ROWS, EDGE_TILES], I32)
        dst_all = sb("dst_all", [EDGE_ROWS, EDGE_TILES], I32)
        gi_src = sb("gi_src", [EDGE_ROWS, 1], I32)
        gi_dst = sb("gi_dst", [EDGE_ROWS, 1], I32)
        gi_put = sb("gi_put", [EDGE_ROWS, 1], I32)
        g_dst = sb("g_dst", [EDGE_ROWS, 1])
        g_dstb = sb("g_dstb", [EDGE_ROWS, EDGE_ROWS])
        g_eq = sb("g_eq", [EDGE_ROWS, EDGE_ROWS])
        g_eql = sb("g_eql", [EDGE_ROWS, EDGE_ROWS])
        g_small = sb("g_small", [EDGE_ROWS, 16])
        g_x = sb("g_x", [EDGE_ROWS, D])
        g_acc = sb("g_acc", [EDGE_ROWS, A])
        g_h = sb("g_h", [EDGE_ROWS, A])
        g_new = sb("g_new", [EDGE_ROWS, A])
        n_acc = sb("n_acc", [NODE_ROWS, A])
        n_x = sb("n_x", [NODE_ROWS, D])
        n_zT = sb("n_zT", [A, NODE_ROWS])
        n_deg = sb("n_deg", [NODE_ROWS, 2])
        n_out = sb("n_out", [NODE_ROWS, D])
        g_loaded = sem("g_loaded")
        g_cleared = sem("g_cleared")
        g_idx = sem("g_idx")
        g_ones = sem("g_ones")
        g_gx = sem("g_gx")
        g_gacc = sem("g_gacc")
        g_chain = sem("g_chain")
        g_dstT = sem("g_dstT")
        g_eqs = sem("g_eqs")
        g_var = sem("g_var")
        g_std = sem("g_std")
        g_scale = sem("g_scale")
        g_hs = sem("g_hs")
        g_sum = sem("g_sum")
        g_news = sem("g_news")
        g_put = sem("g_put")
        n_in = sem("n_in")
        n_T = sem("n_T")
        n_zTs = sem("n_zTs")
        n_mm = sem("n_mm")
        n_chain = sem("n_chain")
        n_done = sem("n_done")
        n_stored = sem("n_stored")
        sp_gate = sem("sp_gate")
        pool_gate = sem("pool_gate")
        dve_gate = sem("dve_gate")

        def iterations(eng, body):
            body(0, True)
            with eng.Fori(1, STEPS // RING) as it:
                body(it, False)

        def edges_broken(eng):
            eng.wait_ge(all_stored, 1)
            eng.wait_ge(flag_ready, 1)
            return eng.value_load(flag_i[0:1, 0:1], min_val=0, max_val=1 << 24)

        block = ctx.enter_context(nc.Block())

        @block.sync
        def _(sp):
            sp.dma_start(e_dst[:, :], dst.rearrange("(p e) -> p e", p=SEG_ROWS)).then_inc(dst_loaded, 16)
            sp.wait_ge(next_set, 2)
            with nc.allow_non_contiguous_dma(reason="three numbers per row"):
                sp.dma_start(e_next[0:SEG_ROWS - 1, :],
                             dst.rearrange("(p s e) -> p s e", s=SEGS, e=SEG)[1:SEG_ROWS, 0:3, 0]
                             ).then_inc(next_loaded, 16)
            sp.dma_start(e_src[:, :], src.rearrange("(p e) -> p e", p=SEG_ROWS)).then_inc(src_loaded, 16)
            sp.dma_start(Waug[0:D, 0:D], W).then_inc(w_loaded, 16)
            sp.dma_start(Waug[D:A, 0:D], b.rearrange("(o d) -> o d", o=1)).then_inc(w_loaded, 16)

            def rows(dram, s):
                first = s * STEP if isinstance(s, int) and s < STEPS - 1 else (
                    N - STEP if isinstance(s, int) else s * STEP)
                return dram[bass.ds(first, STEP), :].rearrange("(w p t) d -> p w (t d)", w=GROUP, t=TILES)

            def load(s, r):
                sp.dma_start(x_in[:, r], rows(x, s)).then_inc(x_loaded[r], 16)

            def store(s, r):
                sp.dma_start(rows(out, s), y[:, r]).then_inc(stored[r], 16)

            load(0, 0)
            load(1, 1)

            def body(it, first):
                for r in range(RING):
                    s = it * RING + r
                    if r > 0 or not first:
                        sp.wait_ge(y_ready, s * 2)
                        store(s - 1, (r - 1) % RING)
                    load(s + 2, (r + 2) % RING)
            body(0, True)
            with sp.Fori(1, STEPS // RING - 1) as it:
                body(it, False)
            for s in range(STEPS - RING, STEPS + 1):
                sp.wait_ge(y_ready, s * 2)
                if s == STEPS:
                    sp.wait_ge(stored[(s - 2) % RING], 16 * ((s - 2) // RING + 1))
                store(s - 1, (s - 1) % RING)
                if s + 2 < STEPS:
                    load(s + 2, (s + 2) % RING)
            for r in range(RING):
                sp.wait_ge(stored[r], 16 * (STEPS // RING))
            sp.sem_inc(all_stored, 1)

            with sp.If(edges_broken(sp) != 0):
                sp.dma_start(src_all[:, :], src.rearrange("(p t) -> p t", p=EDGE_ROWS)).then_inc(g_loaded, 16)
                sp.dma_start(dst_all[:, :], dst.rearrange("(p t) -> p t", p=EDGE_ROWS)).then_inc(g_loaded, 16)
                with sp.Fori(0, 100) as i:
                    sp.dma_start(acc_dram[bass.ds(i * 1000, 1000), :].rearrange("(p r) a -> p (r a)", p=125),
                                 zeros[0:125, 0:8 * A]).then_inc(g_cleared, 16)
                sp.dma_start(acc_dram[N:N + P, :], zeros[:, 0:A]).then_inc(g_cleared, 16)
                sp.wait_ge(g_put, 16 * EDGE_TILES)
                with sp.Fori(0, NODE_TILES) as i:
                    sp.dma_start(n_acc[:, :], acc_dram[bass.ds(i * NODE_ROWS, NODE_ROWS), :]).then_inc(n_in, 16)
                    sp.dma_start(n_x[:, :], x[bass.ds(i * NODE_ROWS, NODE_ROWS), :]).then_inc(n_in, 16)
                    sp.wait_ge(n_done, i + 1)
                    sp.dma_start(out[bass.ds(i * NODE_ROWS, NODE_ROWS), :], n_out[:, :]).then_inc(n_stored, 16)
                    sp.wait_ge(n_stored, i * 16 + 16)
                    sp.sem_inc(sp_gate, 1)
                sp.wait_ge(n_stored, 16 * NODE_TILES)
                sp.sem_inc(sp_gate, 1)

        @block.gpsimd
        def _(pool):
            C = 0

            def link(ins):
                nonlocal C
                C += 1
                ins.then_inc(p_chain, 1)

            link(pool.iota(rev_pos[:, :], [[0, SEGS], [-1, SEG]], base=SEG - 1, channel_multiplier=0,
                           allow_small_or_imprecise_dtypes=True))
            link(pool.iota(head_no[:, :], [[SEG, SEGS + 3]], base=0, channel_multiplier=SEGS * SEG,
                           allow_small_or_imprecise_dtypes=True))
            link(pool.iota(base[:, :], [[TABLE_ROWS, BLOCKS]], base=0, channel_multiplier=1,
                           allow_small_or_imprecise_dtypes=True))
            link(pool.memset(ident[:, :], 0.0))
            pool.wait_ge(p_chain, C)
            pool.affine_select(out=ident[:, :], in_=ident[:, :], compare_op=ALU.not_equal, fill=1.0,
                               base=0, pattern=[[-1, P]], channel_multiplier=1).then_inc(c_pool, 1)
            pool.tensor_scalar(rev_pos[:, :], rev_pos[:, :], float(1 << SRC_BITS), 1.0, ALU.mult,
                               ALU.add).then_inc(c_pool, 1)
            link(pool.tensor_scalar(late[:, :], base[:, :], float(WINDOWS - GROUP), float(-BACK), ALU.is_ge, ALU.mult))
            pool.wait_ge(p_chain, C)
            link(pool.tensor_scalar(base[:, :], base[:, :], float(WINDOW), None, ALU.mult))
            pool.wait_ge(p_chain, C)
            pool.tensor_tensor(base[:, :], base[:, :], late[:, :], ALU.add).then_inc(c_pool, 1)
            pool.iota(own_rows[:, :], [[CAP, SEGS // SPREAD], [0, SPREAD]], base=0, channel_multiplier=LIST_ROWS // 126,
                      allow_small_or_imprecise_dtypes=True).then_inc(c_pool, 1)
            pool.iota(slot_no[:, :, :], [[0, SEGS], [1, CAP]], base=0, channel_multiplier=0,
                      allow_small_or_imprecise_dtypes=True).then_inc(c_pool, 1)
            pool.iota(node_no[:, :, :], [[1, TILES], [TILES, P]], base=0, channel_multiplier=0,
                      allow_small_or_imprecise_dtypes=True).then_inc(c_pool, 1)
            link(pool.memset(later[:, :], 1.0))
            pool.wait_ge(p_chain, C)
            pool.affine_select(out=later[:, :], in_=later[:, :], compare_op=ALU.is_gt, fill=0.0,
                               base=0, pattern=[[1, P]], channel_multiplier=-1).then_inc(c_pool, 1)
            pool.iota(dump_row[:, :], [[0, 1]], base=N, channel_multiplier=1,
                      allow_small_or_imprecise_dtypes=True).then_inc(c_pool, 1)

            pool.wait_ge(chunk_ready, 1)
            for g in range(BLOCKS):
                pool.indirect_dma_start(out=chunk_dst[:, g, :], out_offset=None,
                                        in_=dst.rearrange("(c e) -> c e", e=SEG),
                                        in_offset=bass.IndirectOffsetOnAxis(ap=chunk_i[:, g:g + 1], axis=0)
                                        ).then_inc(chunk_loaded, 16)
            pool.wait_ge(rank_ready, 1)
            pool.wait_ge(pairs_ready, 2)
            for i in range(SPREAD):
                pool.wait_ge(cleared[i], 16)
            for j in range(SEGS):
                pool.indirect_dma_start(out=packed[j % SPREAD],
                                        out_offset=bass.IndirectOffsetOnAxis(ap=rank_i[:, j:j + 1], axis=0),
                                        in_=pairs[:, j].rearrange("p c k -> p (c k)"),
                                        in_offset=None).then_inc(scattered, 16)
            pool.wait_ge(scattered, 16 * SEGS)
            pool.wait_ge(start_ready, 1)
            for g in range(BLOCKS):
                for i in range(SPREAD):
                    pool.indirect_dma_start(out=wpairs[:, g, i, :], out_offset=None, in_=packed[i],
                                            in_offset=bass.IndirectOffsetOnAxis(ap=start_i[:, g:g + 1], axis=0)
                                            ).then_inc(wpairs_loaded[g], 16)

            def body(it, first):
                for r in range(RING):
                    s = it * RING + r
                    if not first:
                        pool.wait_ge(h_ready, (s - RING + 1) * GROUP)
                        pool.sem_inc(pool_gate, 1)
                    pool.wait_ge(idx_ready, s + 1)
                    pool.sem_inc(pool_gate, 1)
                    for t in range(GS):
                        pool.indirect_dma_start(out=x_far[:, r, t, :], out_offset=None, in_=x,
                                                in_offset=bass.IndirectOffsetOnAxis(ap=far_i[:, r, t:t + 1], axis=0)
                                                ).then_inc(gathered[r], 16)
            iterations(pool, body)

            with pool.If(edges_broken(pool) != 0):
                pool.wait_ge(g_cleared, 16 * 101)
                with pool.Fori(0, EDGE_TILES) as i:
                    pool.wait_ge(g_idx, i + 1)
                    pool.sem_inc(pool_gate, 1)
                    pool.indirect_dma_start(out=g_x[:, :], out_offset=None, in_=x,
                                            in_offset=bass.IndirectOffsetOnAxis(ap=gi_src[:, 0:1], axis=0)
                                            ).then_inc(g_gx, 16)
                    pool.indirect_dma_start(out=g_acc[:, :], out_offset=None, in_=acc_dram,
                                            in_offset=bass.IndirectOffsetOnAxis(ap=gi_dst[:, 0:1], axis=0)
                                            ).then_inc(g_gacc, 16)
                    pool.wait_ge(g_news, i + 1)
                    pool.sem_inc(pool_gate, 1)
                    pool.indirect_dma_start(out=acc_dram,
                                            out_offset=bass.IndirectOffsetOnAxis(ap=gi_put[:, 0:1], axis=0),
                                            in_=g_new[:, :], in_offset=None).then_inc(g_put, 16)
                    pool.wait_ge(g_put, i * 16 + 16)
                    pool.sem_inc(pool_gate, 1)
                pool.wait_ge(g_put, 16 * EDGE_TILES)
                pool.sem_inc(pool_gate, 1)

        @block.vector
        def _(dve):
            C = 0

            def link(ins):
                nonlocal C
                C += 1
                ins.then_inc(d_chain, 1)

            def settle():
                dve.wait_ge(d_chain, C)

            dve.memset(e_next[:, 0:1], float(N)).then_inc(next_set, 1)
            dve.memset(e_next[:, 1:3], float(-10 * N)).then_inc(next_set, 1)
            dve.memset(zeros[:, :], 0.0).then_inc(c_dve, 1)
            link(dve.memset(Waug[:, D:A], 0.0))
            settle()
            dve.memset(Waug[D:A, D:A], 1.0).then_inc(c_dve, 1)
            dve.memset(ones[:, :], 1.0).then_inc(c_dve, 1)
            dve.memset(eps[:, :], EPS).then_inc(c_dve, 1)
            dve.memset(h[:, :, :, D:A], 1.0).then_inc(c_dve, 1)
            link(dve.memset(faults[:, :], 0.0))
            link(dve.memset(table[:, STEPS:, :, :], 0.0))

            dve.wait_ge(dst_loaded, 16)
            dve.wait_ge(next_loaded, 16)
            dst_seg = e_dst.rearrange("p (s e) -> p s e", s=SEGS)
            link(dve.tensor_copy(heads[:, 0:SEGS], dst_seg[:, :, 0]))
            link(dve.tensor_copy(heads[:, SEGS:], e_next[:, :]))
            dve.wait_ge(c_pool, 2)
            settle()
            dve.tensor_tensor(head_diag[:, :, :],
                              heads[:, 0:SEGS].rearrange("p (o s) -> p o s", o=1).to_broadcast([SEG_ROWS, SEG_ROWS, SEGS]),
                              ident[0:SEG_ROWS, 0:SEG_ROWS].rearrange("p (q o) -> p q o", o=1).to_broadcast([SEG_ROWS, SEG_ROWS, SEGS]),
                              ALU.mult).then_inc(diag_ready, 1)
            dve.wait_ge(src_loaded, 16)
            link(dve.tensor_tensor(far[:, :], e_src[:, :], e_dst[:, :], ALU.not_equal))
            link(dve.tensor_tensor(same[:, 0:SEGS * SEG - 1], e_dst[:, 0:SEGS * SEG - 1], e_dst[:, 1:SEGS * SEG],
                                   ALU.is_equal))
            link(dve.tensor_tensor(same[:, SEGS * SEG - 1:], e_dst[:, SEGS * SEG - 1:], e_next[:, 0:1], ALU.is_equal))
            key_row = key.rearrange("p s e -> p (s e)")
            link(dve.tensor_tensor(key_row, e_src[:, :], rev_pos[:, :], ALU.add))
            settle()
            link(dve.tensor_tensor(far[:, :], far[:, :], same[:, :], ALU.max))
            settle()
            link(dve.tensor_tensor(key_row, key_row, far[:, :], ALU.mult))

            link(dve.tensor_tensor(rank[:, :], head_no[:, :], heads[:, :], ALU.subtract))
            link(dve.tensor_tensor(same[:, 0:SEGS * SEG - 1], e_dst[:, 0:SEGS * SEG - 1], e_dst[:, 1:SEGS * SEG],
                                   ALU.is_gt))
            link(dve.tensor_tensor(same[:, SEGS * SEG - 1:], e_dst[:, SEGS * SEG - 1:], e_next[:, 0:1], ALU.is_gt))
            settle()
            link(dve.tensor_tensor(gap[:, 0], rank[:, 1:SEGS + 1], rank[:, 0:SEGS], ALU.subtract))
            link(dve.tensor_tensor(gap[:, 1], rank[:, SPREAD:SEGS + SPREAD], rank[:, 0:SEGS], ALU.subtract))
            link(dve.tensor_reduce(faults[0:SEG_ROWS, 0:1], same[:, :], AX.X, ALU.add))
            link(dve.tensor_reduce(faults[0:SEG_ROWS, 9:10], far[:, :], AX.X, ALU.add))
            settle()
            link(dve.tensor_scalar(gap[:, 0], gap[:, 0], float(CAP), None, ALU.is_gt))
            link(dve.tensor_scalar(gap[:, 1], gap[:, 1], float(CAP), None, ALU.is_lt))
            settle()
            link(dve.tensor_reduce(faults[0:SEG_ROWS, 1:3], gap[:, :, :], AX.X, ALU.add))
            settle()
            dve.sem_inc(tests_ready, 1)

            dve.wait_ge(heads_spread, 3)
            dve.wait_ge(c_pool, 3)
            third = SEG_ROWS * SEGS // 3
            for g in range(BLOCKS):
                link(dve.tensor_scalar(below.rearrange("p (k n) -> p k n", k=3),
                                       ps[0:TABLE_ROWS, 0:3, 0:third], base[:, g:g + 1], None, ALU.is_lt))
                settle()
                link(dve.tensor_reduce(chunk[:, g:g + 1], below[:, :], AX.X, ALU.add))
                settle()
            link(dve.tensor_scalar(chunk[:, :], chunk[:, :], -1.0, 0.0, ALU.add, ALU.max))
            settle()
            dve.tensor_copy(chunk_i[:, :], chunk[:, :]).then_inc(chunk_ready, 1)

            for k in range(ROUNDS):
                for j in range(SEGS):
                    link(dve.max(found[:, j, 8 * k:8 * k + 8], key[:, j, :]))
                settle()
                if k < ROUNDS - 1:
                    for j in range(SEGS):
                        link(dve.match_replace(out=key[:, j, :], in_to_replace=found[:, j, 8 * k:8 * k + 8],
                                               in_values=key[:, j, :], imm_value=0.0))
                    settle()
            dve.wait_ge(tests_summed, 1)
            dve.wait_ge(c_pool, 5)
            link(dve.tensor_reduce(fine[:, 0:1], ps[0:SEG_ROWS, 3, 0:3], AX.X, ALU.add))
            link(dve.tensor_scalar(fine[:, 1:2], ps[0:SEG_ROWS, 3, 9:10], float(FAR), None, ALU.is_equal))
            link(dve.tensor_tensor(rank[:, 0:SEGS], rank[:, 0:SEGS], own_rows[:, :], ALU.subtract))
            settle()
            link(dve.scalar_tensor_tensor(out=fine[:, 2:3], in0=fine[:, 0:1], scalar=0.0, in1=fine[:, 1:2],
                                          op0=ALU.is_equal, op1=ALU.mult))
            settle()
            dve.scalar_tensor_tensor(out=rank_i[:, :], in0=rank[:, 0:SEGS], scalar=fine[:, 2:3], in1=own_rows[:, :],
                                     op0=ALU.mult, op1=ALU.add).then_inc(rank_ready, 1)
            link(dve.tensor_scalar(found_i[:, :, :], found[:, :, :], -1.0, None, ALU.add))
            link(dve.tensor_scalar(valid[:, :, :], found[:, :, :], 0.5, None, ALU.is_gt))
            dve.wait_ge(c_pool, 5)
            settle()
            link(dve.tensor_scalar(part_i[:, 0], found_i[:, :, :], (1 << SRC_BITS) - 1, None, ALU.bitwise_and))
            link(dve.tensor_scalar(part_i[:, 1], found_i[:, :, :], SRC_BITS, None, ALU.arith_shift_right))
            link(dve.tensor_tensor(tgt[:, :, :], heads[:, 0:SEGS].rearrange("p (s o) -> p s o", o=1).to_broadcast([SEG_ROWS, SEGS, CAP]),
                                   slot_no[:, :, :], ALU.subtract))
            settle()
            dve.tensor_tensor(pairs[:, :, :, 0], part_i[:, 0], valid[:, :, :], ALU.mult).then_inc(pairs_ready, 1)
            link(dve.scalar_tensor_tensor(out=tgt[:, :, :], in0=tgt[:, :, :], scalar=float(SEG - 1), in1=part_i[:, 1],
                                          op0=ALU.add, op1=ALU.subtract))
            settle()
            dve.tensor_tensor(pairs[:, :, :, 1], tgt[:, :, :], valid[:, :, :], ALU.mult).then_inc(pairs_ready, 1)

            dve.wait_ge(chunk_loaded, 16 * BLOCKS)
            for g in range(BLOCKS):
                link(dve.tensor_scalar(below_c[:, g, :], chunk_dst[:, g, :], base[:, g:g + 1], None, ALU.is_lt))
            settle()
            link(dve.tensor_reduce(start[:, :], below_c[:, :, :], AX.X, ALU.add))
            settle()
            link(dve.scalar_tensor_tensor(out=start[:, :], in0=chunk[:, :], scalar=float(SEG), in1=start[:, :],
                                          op0=ALU.mult, op1=ALU.add))
            settle()
            link(dve.tensor_tensor(start[:, :], start[:, :], base[:, :], ALU.subtract))
            settle()
            link(dve.tensor_scalar(start[:, :], start[:, :], 0.0, float(FAR), ALU.max, ALU.min))
            settle()
            dve.tensor_copy(start_i[:, :], start[:, :]).then_inc(start_ready, 1)

            for g in range(BLOCKS):
                dve.wait_ge(wpairs_loaded[g], 16 * SPREAD)
                link(dve.tensor_tensor(wpairs[:, g, 0], wpairs[:, g, 0], wpairs[:, g, 1], ALU.add))
                settle()
                link(dve.tensor_tensor(wpairs[:, g, 0], wpairs[:, g, 0], wpairs[:, g, 2], ALU.add))
                settle()
                got = wpairs[:, g, 0].rearrange("p (c k) -> p k c", k=2)
                link(dve.tensor_scalar(wedge[:, g, 0, :], got[:, 0, :], 0.0, float(N - 1), ALU.max, ALU.min))
                link(dve.tensor_scalar(wedge[:, g, 1, :], got[:, 1, :], base[:, g:g + 1], None, ALU.subtract))
                link(dve.tensor_scalar(wtest[:, g, 0:1], start[:, g:g + 1], float(FAR - PACKED), None, ALU.is_lt))
                link(dve.tensor_scalar(wtest[:, g, 1:2], start[:, g:g + 1], float(FAR - P), None, ALU.is_lt))
                settle()
                link(dve.scalar_tensor_tensor(out=faults[0:TABLE_ROWS, 3 + 2 * g:4 + 2 * g],
                                              in0=wedge[:, g, 1, PACKED:PACKED + 1], scalar=float(WINDOW),
                                              in1=wtest[:, g, 0:1], op0=ALU.is_lt, op1=ALU.mult))
                link(dve.scalar_tensor_tensor(out=faults[0:TABLE_ROWS, 4 + 2 * g:5 + 2 * g],
                                              in0=wedge[:, g, 1, P:P + 1], scalar=float(TILES * SKIP),
                                              in1=wtest[:, g, 1:2], op0=ALU.is_lt, op1=ALU.mult))
                dve.sem_inc(wedge_ready, 1)
                dve.wait_ge(turned, 2 * SLOTS * (g + 1))
                for kind in range(2):
                    for t in range(SLOTS):
                        link(dve.tensor_copy(
                            table[:, g * BLOCK_STEPS:(g + 1) * BLOCK_STEPS, kind, :]
                            .rearrange("p s (w t) -> p s w t", t=SLOTS)[:, :, :, t],
                            ps[:, 4 + kind * SLOTS + t, 0:TABLE_ROWS].rearrange("p (s w) -> p s w", w=GROUP)))
                settle()
                dve.sem_inc(turned_used, 1)
            link(dve.tensor_reduce(flag[:, 0:1], faults[:, 0:9], AX.X, ALU.add))
            settle()
            link(dve.tensor_copy(flag[:, 1:2], faults[:, 9:10]))
            settle()
            dve.sem_inc(faults_ready, 1)
            dve.wait_ge(faults_summed, 1)
            link(dve.tensor_scalar(flag[0:1, 2:3], ps[0:1, 0, 1:2], float(FAR), None, ALU.not_equal))
            settle()
            link(dve.tensor_tensor(flag[0:1, 3:4], ps[0:1, 0, 0:1], flag[0:1, 2:3], ALU.add))
            settle()
            dve.tensor_copy(flag_i[:, :], flag[0:1, 3:4]).then_inc(flag_ready, 1)

            def indices(s, r):
                dve.tensor_copy(far_n[:, r, :], table[:, bass.ds(s, 1), 1, :]).then_inc(s_chain, 1)
                dve.tensor_copy(far_i[:, r, :], table[:, bass.ds(s, 1), 0, :]).then_inc(idx_ready, 1)

            indices(0, 0)
            indices(1, 1)
            K = 7

            def statistics(it, r, first):
                s = it * RING + r
                c = s * K + 2
                dve.wait_ge(x_loaded[r], it * 16 + 16)
                for w in range(GROUP):
                    for t in range(TILES):
                        dve.bn_stats(stats[:, r, w * TILES + t, :], x_in[:, r, w, t * D:t * D + D])
                dve.wait_ge(gathered[r], it * (16 * GS) + 16 * GS)
                for t in range(GS):
                    last = dve.bn_stats(stats[:, r, GT + t, :], x_far[:, r, t, :])
                last.then_inc(s_chain, 1)
                c = c + 1
                dve.wait_ge(s_chain, c)
                S, L = stats[:, r], ln[:, r]
                dve.tensor_tensor(L[:, 0], S[:, :, 1], S[:, :, 4], ALU.subtract).then_inc(s_chain, 1)
                dve.tensor_tensor(L[:, 1], S[:, :, 2], S[:, :, 5], ALU.add).then_inc(s_chain, 1)
                dve.tensor_tensor(L[:, 2], S[:, :, 1], S[:, :, 4], ALU.add).then_inc(s_chain, 1)
                dve.wait_ge(s_chain, c + 3)
                dve.tensor_tensor(L[:, 3], L[:, 0], L[:, 0], ALU.mult).then_inc(s_chain, 1)
                dve.wait_ge(s_chain, c + 4)
                dve.scalar_tensor_tensor(out=L[:, 4], in0=L[:, 3], scalar=float(D) / 4, in1=L[:, 1],
                                         op0=ALU.mult, op1=ALU.add).then_inc(var_ready, 1)

            def hits(it, r, first):
                s = it * RING + r
                if not first:
                    dve.wait_ge(z_ready, (s - RING + 1) * GROUP)
                for w in range(GROUP):
                    dve.tensor_scalar(hit0[:, r, w], node_no[:, :, :], far_n[:, r, SLOTS * w:SLOTS * w + 1], None,
                                      ALU.is_equal)
                    dve.tensor_scalar(hit1[:, r, w], node_no[:, :, SKIP:], far_n[:, r, SLOTS * w + 1:SLOTS * w + 2],
                                      None, ALU.is_equal).then_inc(hits_ready, 1)

            def scales(it, r):
                s = it * RING + r
                c = s * K + 2 + 5
                dve.wait_ge(std_ready, s + 1)
                L = ln[:, r]
                dve.reciprocal(L[:, 6], L[:, 5]).then_inc(s_chain, 1)
                dve.wait_ge(s_chain, c + 1)
                dve.scalar_tensor_tensor(out=L[:, 7], in0=L[:, 2], scalar=-0.5, in1=L[:, 6],
                                         op0=ALU.mult, op1=ALU.mult).then_inc(ln_ready, 1)

            def finish(it, r, first):
                s = it * RING + r
                if not first:
                    dve.wait_ge(stored[r], it * 16)
                for half in range(2):
                    w0 = half * (GROUP // 2)
                    dve.wait_ge(m_ready, s * GROUP + w0 + GROUP // 2)
                    M = ps[:, 4 + w0:4 + w0 + GROUP // 2, 0:TILES * A].rearrange("p w (t a) -> p w t a", t=TILES)
                    R = recip[:, half]
                    dve.reciprocal(R, M[:, :, :, D]).then_inc(f_chain, 1)
                    dve.wait_ge(f_chain, s * 2 + half + 1)
                    dve.tensor_tensor(scaled[:, half], M[:, :, :, 0:D],
                                      R.rearrange("p w (t o) -> p w t o", o=1).to_broadcast([P, GROUP // 2, TILES, D]),
                                      ALU.mult).then_inc(f_read, 1)
                    dve.wait_ge(f_read, s * 2 + half + 1)
                    dve.tensor_tensor(y[:, r, w0:w0 + GROUP // 2],
                                      scaled[:, half].rearrange("p w t d -> p w (t d)"),
                                      x_in[:, r, w0:w0 + GROUP // 2], ALU.add).then_inc(y_ready, 1)

            def body(it, first):
                for r in range(RING):
                    s = it * RING + r
                    statistics(it, r, first)
                    hits(it, r, first)
                    scales(it, r)
                    if r > 0:
                        finish(it, r - 1, first)
                    elif not first:
                        finish(it - 1, RING - 1, isinstance(it, int) and it == 1)
                    indices(s + 2, (r + 2) % RING)
            if True:
                body(0, True)
                body(1, False)
                with dve.Fori(2, STEPS // RING) as it:
                    body(it, False)
                finish(STEPS // RING - 1, RING - 1, False)

            with dve.If(edges_broken(dve) != 0):
                dve.memset(g_h[:, D:A], 1.0).then_inc(g_ones, 1)
                dve.wait_ge(g_loaded, 32)
                with dve.Fori(0, EDGE_TILES) as i:
                    c = i * 9
                    dve.tensor_copy(gi_src[:, :], src_all[:, bass.ds(i, 1)]).then_inc(g_chain, 1)
                    dve.tensor_copy(gi_dst[:, :], dst_all[:, bass.ds(i, 1)]).then_inc(g_chain, 1)
                    dve.tensor_copy(g_dst[:, :], dst_all[:, bass.ds(i, 1)]).then_inc(g_chain, 1)
                    dve.wait_ge(g_chain, c + 3)
                    dve.tensor_copy(g_dstb[:, :], g_dst[:, 0:1].to_broadcast([EDGE_ROWS, EDGE_ROWS])).then_inc(g_idx, 1)
                    dve.wait_ge(g_dstT, i + 1)
                    dve.tensor_scalar(g_eq[:, :], ps[0:EDGE_ROWS, 0, 0:EDGE_ROWS], g_dst[:, 0:1], None,
                                      ALU.is_equal).then_inc(g_eqs, 1)
                    dve.wait_ge(g_eqs, i + 1)
                    dve.tensor_tensor_reduce(out=g_eql[:, :], in0=g_eq[:, :], in1=later[0:EDGE_ROWS, 0:EDGE_ROWS],
                                             scale=1.0, scalar=0.0, op0=ALU.mult, op1=ALU.add,
                                             accum_out=g_small[:, 8:9]).then_inc(g_chain, 1)
                    dve.wait_ge(g_chain, c + 4)
                    dve.tensor_scalar(g_small[:, 9:10], g_small[:, 8:9], 1.0, None, ALU.min).then_inc(g_chain, 1)
                    dve.tensor_tensor(g_small[:, 10:11], dump_row[0:EDGE_ROWS, :], g_dst[:, 0:1],
                                      ALU.subtract).then_inc(g_chain, 1)
                    dve.wait_ge(g_chain, c + 6)
                    dve.scalar_tensor_tensor(out=gi_put[:, :], in0=g_small[:, 10:11], scalar=g_small[:, 9:10],
                                             in1=g_dst[:, :], op0=ALU.mult, op1=ALU.add).then_inc(g_chain, 1)
                    dve.wait_ge(g_gx, i * 16 + 16)
                    dve.bn_stats(g_small[:, 0:6], g_x[:, :]).then_inc(g_chain, 1)
                    dve.wait_ge(g_chain, c + 8)
                    dve.sem_inc(dve_gate, 1)
                    dve.bn_aggr(g_small[:, 11:13], g_small[:, 0:6]).then_inc(g_chain, 1)
                    dve.wait_ge(g_chain, c + 9)
                    dve.tensor_scalar(g_small[:, 13:14], g_small[:, 12:13], EPS, None, ALU.add).then_inc(g_var, 1)
                    dve.wait_ge(g_std, i + 1)
                    dve.reciprocal(g_small[:, 15:16], g_small[:, 14:15]).then_inc(g_scale, 1)
                    dve.wait_ge(g_scale, i * 2 + 1)
                    dve.scalar_tensor_tensor(out=g_small[:, 8:9], in0=g_small[:, 11:12], scalar=-1.0,
                                             in1=g_small[:, 15:16], op0=ALU.mult, op1=ALU.mult).then_inc(g_scale, 1)
                    dve.wait_ge(g_sum, i + 1)
                    dve.wait_ge(g_gacc, i * 16 + 16)
                    dve.tensor_tensor(g_new[:, :], ps[0:EDGE_ROWS, 1, 0:A], g_acc[:, :], ALU.add).then_inc(g_news, 1)
                    dve.wait_ge(g_put, i * 16 + 16)
                    dve.sem_inc(dve_gate, 1)
                with dve.Fori(0, NODE_TILES) as i:
                    dve.wait_ge(n_T, i + 1)
                    dve.tensor_copy(n_zT[:, :], ps[0:A, 2, 0:NODE_ROWS]).then_inc(n_zTs, 1)
                    dve.wait_ge(n_mm, i + 1)
                    dve.tensor_scalar(n_deg[:, 0:1], ps[0:NODE_ROWS, 3, D:A], 1.0, None, ALU.max).then_inc(n_chain, 1)
                    dve.wait_ge(n_chain, i * 2 + 1)
                    dve.reciprocal(n_deg[:, 1:2], n_deg[:, 0:1]).then_inc(n_chain, 1)
                    dve.wait_ge(n_chain, i * 2 + 2)
                    dve.scalar_tensor_tensor(out=n_out[:, :], in0=ps[0:NODE_ROWS, 3, 0:D], scalar=n_deg[:, 1:2],
                                             in1=n_x[:, :], op0=ALU.mult, op1=ALU.add).then_inc(n_done, 1)

        @block.scalar
        def _(act):
            act.wait_ge(c_dve, 1)
            for i in range(SPREAD):
                act.dma_start(packed[i].rearrange("(p r) k -> p (r k)", p=126),
                              zeros[0:126, :]).then_inc(cleared[i], 16)
            act.wait_ge(c_dve, 5)

            def copy_zT(s, w, first):
                act.wait_ge(z_ready, s * GROUP + w + 1)
                if not first:
                    act.wait_ge(m_ready, (s - 1) * GROUP + w + 1)
                act.activation(zT[:, w, :], ps[0:A, w, 0:WINDOW], ACT.Copy).then_inc(zT_ready, 1)

            def body(it, first):
                for r in range(RING):
                    s = it * RING + r
                    S, L = stats[:, r], ln[:, r]
                    act.wait_ge(var_ready, s + 1)
                    act.activation(L[:, 5], L[:, 4], ACT.Sqrt, bias=eps[:, :], scale=1.0 / D).then_inc(std_ready, 1)
                    if not first:
                        act.wait_ge(z_ready, (s - RING + 1) * GROUP)
                    act.wait_ge(ln_ready, s + 1)
                    for w in range(GROUP):
                        for t in range(TILES):
                            k = w * TILES + t
                            act.activation(h[:, r, k, 0:D], x_in[:, r, w, t * D:t * D + D], ACT.Relu,
                                           bias=L[:, 7, k:k + 1], scale=L[:, 6, k:k + 1])
                        for t in range(SLOTS):
                            k = GT + w * SLOTS + t
                            last = act.activation(h[:, r, k, 0:D], x_far[:, r, w * SLOTS + t, :], ACT.Relu,
                                                  bias=L[:, 7, k:k + 1], scale=L[:, 6, k:k + 1])
                        last.then_inc(h_ready, 1)
                        if w > 0:
                            copy_zT(s, w - 1, first and r == 0)
                        elif r > 0 or not first:
                            copy_zT(s - 1, GROUP - 1, first and r == 1)
            iterations(act, body)
            copy_zT(STEPS - 1, GROUP - 1, False)

            with act.If(edges_broken(act) != 0):
                with act.Fori(0, EDGE_TILES) as i:
                    act.wait_ge(g_var, i + 1)
                    act.activation(g_small[:, 14:15], g_small[:, 13:14], ACT.Sqrt).then_inc(g_std, 1)
                    act.wait_ge(g_scale, i * 2 + 2)
                    act.activation(g_h[:, 0:D], g_x[:, :], ACT.Relu, bias=g_small[:, 8:9],
                                   scale=g_small[:, 15:16]).then_inc(g_hs, 1)

        @block.tensor
        def _(pe):
            pe.wait_ge(c_dve, 5)
            pe.wait_ge(w_loaded, 32)
            pe.wait_ge(c_pool, 8)
            pe.wait_ge(diag_ready, 1)
            third = SEG_ROWS * SEGS // 3
            hd = head_diag.rearrange("p q s -> p (q s)")
            for k in range(3):
                pe.matmul(ps[0:TABLE_ROWS, k, 0:third], ones[0:SEG_ROWS, 0:TABLE_ROWS],
                          hd[:, k * third:(k + 1) * third], start=True, stop=True).then_inc(heads_spread, 1)
            pe.wait_ge(tests_ready, 1)
            pe.matmul(ps[0:SEG_ROWS, 3, 0:10], ones[0:SEG_ROWS, 0:SEG_ROWS], faults[0:SEG_ROWS, :],
                      start=True, stop=True).then_inc(tests_summed, 1)
            for g in range(BLOCKS):
                pe.wait_ge(wedge_ready, g + 1)
                if g > 0:
                    pe.wait_ge(turned_used, g)
                for kind in range(2):
                    for t in range(SLOTS):
                        pe.transpose(ps[:, 4 + kind * SLOTS + t, 0:TABLE_ROWS], wedge[:, g, kind, t * P:(t + 1) * P],
                                     ident[0:TABLE_ROWS, 0:TABLE_ROWS]).then_inc(turned, 1)
            pe.wait_ge(faults_ready, 1)
            pe.matmul(ps[0:1, 0, 0:2], ones[:, 0:1], flag[:, 0:2], start=True, stop=True).then_inc(faults_summed, 1)
            pe.wait_ge(flag_ready, 1)

            def sums(s, r, w, first):
                pe.wait_ge(h_ready, s * GROUP + w + 1)
                pe.wait_ge(hits_ready, s * GROUP + w + 1)
                if not first:
                    pe.wait_ge(zT_ready, (s - 1) * GROUP + w + 1)
                for t in range(TILES):
                    pe.matmul(ps[0:A, w, t * P:(t + 1) * P], h[:, r, w * TILES + t, :], ident[:, :],
                              start=(t == 0), stop=False, is_transpose=True)
                pe.matmul(ps[0:A, w, 0:WINDOW], h[:, r, GT + w * SLOTS, :], hit0[:, r, w].rearrange("p t n -> p (t n)"),
                          start=False, stop=False)
                pe.matmul(ps[0:A, w, 0:WINDOW].rearrange("p (t n) -> p t n", t=TILES)[:, :, SKIP:],
                          h[:, r, GT + w * SLOTS + 1, :], hit1[:, r, w], start=False, stop=True).then_inc(z_ready, 1)

            def product(s, w, first):
                pe.wait_ge(zT_ready, s * GROUP + w + 1)
                if not first:
                    pe.wait_ge(f_read, (s - 1) * 2 + w // 2 + 1)
                for t in range(TILES):
                    last = pe.matmul(ps[:, 4 + w, t * A:(t + 1) * A], zT[:, w, t * P:(t + 1) * P], Waug[:, :],
                                     start=True, stop=True)
                last.then_inc(m_ready, 1)

            def body(it, first):
                for r in range(RING):
                    s = it * RING + r
                    for w in range(GROUP):
                        sums(s, r, w, first and r == 0)
                        if w > 0:
                            product(s, w - 1, first and r == 0)
                        elif r > 0 or not first:
                            product(s - 1, GROUP - 1, first and r == 1)
            iterations(pe, body)
            product(STEPS - 1, GROUP - 1, False)

            with pe.If(edges_broken(pe) != 0):
                pe.wait_ge(g_ones, 1)
                with pe.Fori(0, EDGE_TILES) as i:
                    pe.wait_ge(g_idx, i + 1)
                    pe.transpose(ps[0:EDGE_ROWS, 0, 0:EDGE_ROWS], g_dstb[:, :],
                                 ident[0:EDGE_ROWS, 0:EDGE_ROWS]).then_inc(g_dstT, 1)
                    pe.wait_ge(g_eqs, i + 1)
                    pe.wait_ge(g_hs, i + 1)
                    pe.matmul(ps[0:EDGE_ROWS, 1, 0:A], g_eq[:, :], g_h[:, :], start=True, stop=True).then_inc(g_sum, 1)
                with pe.Fori(0, NODE_TILES) as i:
                    pe.wait_ge(n_in, i * 32 + 32)
                    pe.transpose(ps[0:A, 2, 0:NODE_ROWS], n_acc[:, :],
                                 ident[0:NODE_ROWS, 0:NODE_ROWS]).then_inc(n_T, 1)
                    pe.wait_ge(n_zTs, i + 1)
                    pe.matmul(ps[0:NODE_ROWS, 3, 0:A], n_zT[:, :], Waug[:, :], start=True, stop=True).then_inc(n_mm, 1)


_INS = ["x", "src", "dst", "L0_gnn_W", "L0_gnn_b"]


def kernel(**inputs):
    import numpy as _np
    import concourse.bacc as _bacc
    from concourse import mybir as _mybir
    from concourse.bass_utils import run_bass_kernel_spmd as _run

    nc = _bacc.Bacc("TRN2", target_bir_lowering=False, num_devices=1)
    arrays, args = {}, []
    for name in _INS:
        a = _np.ascontiguousarray(inputs[name])
        arrays[f"in_{name}_dram"] = a
        args.append(nc.dram_tensor(f"in_{name}_dram", a.shape, _mybir.dt.from_np(a.dtype), kind="ExternalInput").ap())
    args.append(nc.dram_tensor("out_0_dram", inputs["x"].shape, _mybir.dt.float32, kind="ExternalOutput").ap())
    gnn_layer(nc, *args)
    r = _run(nc, [arrays], core_ids=[0])
    return r.results[0]["out_0_dram"]
```

```python
from contextlib import ExitStack

import concourse.bass as bass
from concourse import mybir

ALU = mybir.AluOpType
ACT = mybir.ActivationFunctionType
AX = mybir.AxisListType
F32 = mybir.dt.float32
I32 = mybir.dt.int32

P = 128
EPS = 1e-5

SEG_ROWS = 125
SEGS = 12
SEG = 100
CAP = 56
ROUNDS = CAP // 8
BATCHES = ((0, 6), (6, 9), (9, 12))
BANK_SEGS = 4
SPREAD = 3
SRC_BITS = 17

TILES = 3
WINDOW = TILES * P
SLOTS = 2
GROUP = 4
SKIP = 56
DVE_COPY = 1
RING = 3
TABLE_ROWS = 88

EDGE_ROWS = 120
NODE_ROWS = 125


def gnn_layer(nc, x, src, dst, W, b, out):
    N, D = x.shape
    E = src.shape[0]
    A = D + 1
    FAR = E - N
    assert SEG_ROWS * SEGS * SEG == E and N < 1 << SRC_BITS and (SEG + 1) << SRC_BITS <= 1 << 24

    STEP = GROUP * WINDOW
    STEPS = -(-N // STEP)
    BACK = STEPS * STEP - N
    WINDOWS = STEPS * GROUP
    BLOCKS = WINDOWS // TABLE_ROWS
    BLOCK_STEPS = TABLE_ROWS // GROUP
    assert BLOCKS * TABLE_ROWS == WINDOWS and STEPS % RING == 0
    PACKED = SLOTS * P
    LIST_ROWS = 126 * 400
    assert LIST_ROWS >= FAR + PACKED + 1
    GT = GROUP * TILES
    GS = GROUP * SLOTS
    LN = GT + GS
    LATE = P - SKIP

    EDGE_TILES = E // EDGE_ROWS
    NODE_TILES = N // NODE_ROWS
    assert EDGE_TILES * EDGE_ROWS == E and NODE_TILES * NODE_ROWS == N

    with ExitStack() as ctx:
        def sb(name, shape, dt=F32):
            return ctx.enter_context(nc.sbuf_tensor(name, shape, dt))

        def sem(name):
            return ctx.enter_context(nc.semaphore(name))

        ps = ctx.enter_context(nc.psum_tensor("ps", [P, 8, 512], F32))

        ident = sb("ident", [P, P])
        later = sb("later", [P, P])
        node_no = sb("node_no", [P, TILES, P])
        node_late = sb("node_late", [P, LATE * TILES])
        Waug = sb("Waug", [A, A])
        ones = sb("ones", [P, P])
        eps = sb("eps", [P, 1])
        dump_row = sb("dump_row", [P, 1])
        zeros = sb("zeros", [P, 800])
        c_pool = sem("c_pool")
        c_dve = sem("c_dve")
        w_loaded = sem("w_loaded")

        x_in = sb("x_in", [P, RING, GROUP, TILES * D])
        x_far = sb("x_far", [P, RING, GS, D])
        far_i = sb("far_i", [P, RING, GS], I32)
        far_n = sb("far_n", [P, RING, GS])
        stats = sb("stats", [P, RING, LN, 3])
        ln = sb("ln", [P, RING, 3, LN])
        h = sb("h", [P, RING, LN, A])
        hit0 = sb("hit0", [P, RING, GROUP, TILES, P])
        hit1 = sb("hit1", [P, RING, GROUP, LATE * TILES])
        zT = sb("zT", [A, GROUP, WINDOW])
        recip = sb("recip", [P, 2, GROUP // 2, TILES])
        scaled = sb("scaled", [P, 2, GROUP // 2, TILES, D])
        y = sb("y", [P, RING, GROUP, TILES * D])

        x_loaded = [[sem(f"x_loaded{i}_{half}") for half in range(2)] for i in range(RING)]
        stored = [sem(f"stored{i}") for i in range(RING)]
        gathered = [sem(f"gathered{i}") for i in range(RING)]
        idx_ready = sem("idx_ready")
        ln_chain = sem("ln_chain")
        far_ready = sem("far_ready")
        stats_ready = sem("stats_ready")
        std_ready = sem("std_ready")
        ln_ready = sem("ln_ready")
        hits_ready = sem("hits_ready")
        h_ready = sem("h_ready")
        z_ready = sem("z_ready")
        zT_ready = sem("zT_ready")
        zT_copied = sem("zT_copied")
        m_ready = sem("m_ready")
        f_chain = sem("f_chain")
        f_read = sem("f_read")
        y_ready = sem("y_ready")
        all_stored = sem("all_stored")

        src_table = sb("src_table", [P, STEPS + RING, GS], I32)
        tgt_table = sb("tgt_table", [P, STEPS + RING, GS])
        flag = sb("flag", [P, 4])
        flag_i = sb("flag_i", [1, 1], I32)

        early = ExitStack()

        def early_sb(name, shape, dt=F32):
            return early.enter_context(nc.sbuf_tensor(name, shape, dt))

        packed = [nc.dram_tensor(f"packed{i}", [LIST_ROWS, 2], F32).ap() for i in range(SPREAD)]
        e_src = early_sb("e_src", [SEG_ROWS, SEGS * SEG], I32)
        e_dst = early_sb("e_dst", [SEG_ROWS, SEGS * SEG], I32)
        e_next = early_sb("e_next", [SEG_ROWS, 3], I32)
        key = early_sb("key", [SEG_ROWS, SEGS, SEG])
        far = early_sb("far", [SEG_ROWS, SEGS * SEG])
        ahead = early_sb("ahead", [SEG_ROWS, SEGS * SEG], I32)
        rev_pos = early_sb("rev_pos", [SEG_ROWS, SEG])
        found = early_sb("found", [SEG_ROWS, SEGS, CAP])
        found_i = early_sb("found_i", [SEG_ROWS, SEGS, CAP], I32)
        part_i = early_sb("part_i", [SEG_ROWS, 2, SEGS, CAP], I32)
        place = early_sb("place", [SEG_ROWS, SEGS, CAP])
        valid = early_sb("valid", [SEG_ROWS, SEGS, CAP])
        slot_no = early_sb("slot_no", [SEG_ROWS, CAP])
        tgt = early_sb("tgt", [SEG_ROWS, SEGS, CAP])
        pairs = early_sb("pairs", [SEG_ROWS, SEGS, CAP, 2])
        heads = early_sb("heads", [SEG_ROWS, SEGS + 3])
        head_no = early_sb("head_no", [SEG_ROWS, SEGS + 3])
        rank = early_sb("rank", [SEG_ROWS, SEGS + 3])
        rank_i = early_sb("rank_i", [SEG_ROWS, SEGS], I32)
        own_rows = early_sb("own_rows", [SEG_ROWS, SEGS])
        fine = early_sb("fine", [SEG_ROWS, 3])
        gap = early_sb("gap", [SEG_ROWS, 2, SEGS])
        faults = early_sb("faults", [P, 10])
        signs = early_sb("signs", [TABLE_ROWS, BLOCKS, SEGS * SEG_ROWS], mybir.dt.bfloat16)
        sign_sum = early_sb("sign_sum", [TABLE_ROWS, BLOCKS])
        base_less = early_sb("base_less", [TABLE_ROWS, BLOCKS])
        spare = early_sb("spare", [SEG_ROWS, 2, SEGS * SEG], mybir.dt.bfloat16)
        below_c = early_sb("below_c", [TABLE_ROWS, BLOCKS, SEG])
        base = early_sb("base", [TABLE_ROWS, BLOCKS])
        late = early_sb("late", [TABLE_ROWS, BLOCKS])
        chunk = early_sb("chunk", [TABLE_ROWS, BLOCKS])
        chunk_i = early_sb("chunk_i", [TABLE_ROWS, BLOCKS], I32)
        chunk_dst = early_sb("chunk_dst", [TABLE_ROWS, BLOCKS, SEG], I32)
        start = early_sb("start", [TABLE_ROWS, BLOCKS])
        start_i = early_sb("start_i", [TABLE_ROWS, BLOCKS], I32)
        wpairs = early_sb("wpairs", [TABLE_ROWS, BLOCKS, SPREAD, (PACKED + 1) * 2])
        wedge = early_sb("wedge", [TABLE_ROWS, BLOCKS, 2, PACKED + 1])
        wtest = early_sb("wtest", [TABLE_ROWS, BLOCKS, 4])

        dst_loaded = sem("dst_loaded")
        src_loaded = sem("src_loaded")
        next_set = sem("next_set")
        next_loaded = sem("next_loaded")
        cleared = [sem(f"cleared{i}") for i in range(SPREAD)]
        rank_ready = sem("rank_ready")
        tests_ready = sem("tests_ready")
        tests_summed = sem("tests_summed")
        picked = sem("picked")
        placed = sem("placed")
        tgt_ready = sem("tgt_ready")
        pairs_ready = sem("pairs_ready")
        scattered = sem("scattered")
        heads_ready = sem("heads_ready")
        ahead_ready = sem("ahead_ready")
        far_found = sem("far_found")
        counted = sem("counted")
        summed = sem("summed")
        heads_spread = sem("heads_spread")
        chunk_ready = sem("chunk_ready")
        chunk_loaded = sem("chunk_loaded")
        start_ready = sem("start_ready")
        wpairs_loaded = [sem(f"wpairs_loaded{i}") for i in range(BLOCKS)]
        wedge_ready = sem("wedge_ready")
        turned = sem("turned")
        table_ready = sem("table_ready")
        faults_ready = sem("faults_ready")
        faults_summed = sem("faults_summed")
        flag_ready = sem("flag_ready")
        d_chain = sem("d_chain")
        p_chain = sem("p_chain")

        early.close()
        acc_dram = nc.dram_tensor("acc_dram", [N + P, A], F32).ap()
        src_all = sb("src_all", [EDGE_ROWS, EDGE_TILES], I32)
        dst_all = sb("dst_all", [EDGE_ROWS, EDGE_TILES], I32)
        gi_src = sb("gi_src", [EDGE_ROWS, 1], I32)
        gi_dst = sb("gi_dst", [EDGE_ROWS, 1], I32)
        gi_put = sb("gi_put", [EDGE_ROWS, 1], I32)
        g_dst = sb("g_dst", [EDGE_ROWS, 1])
        g_dstb = sb("g_dstb", [EDGE_ROWS, EDGE_ROWS])
        g_eq = sb("g_eq", [EDGE_ROWS, EDGE_ROWS])
        g_eql = sb("g_eql", [EDGE_ROWS, EDGE_ROWS])
        g_small = sb("g_small", [EDGE_ROWS, 16])
        g_x = sb("g_x", [EDGE_ROWS, D])
        g_acc = sb("g_acc", [EDGE_ROWS, A])
        g_h = sb("g_h", [EDGE_ROWS, A])
        g_new = sb("g_new", [EDGE_ROWS, A])
        n_acc = sb("n_acc", [NODE_ROWS, A])
        n_x = sb("n_x", [NODE_ROWS, D])
        n_zT = sb("n_zT", [A, NODE_ROWS])
        n_deg = sb("n_deg", [NODE_ROWS, 2])
        n_out = sb("n_out", [NODE_ROWS, D])
        g_loaded = sem("g_loaded")
        g_cleared = sem("g_cleared")
        g_idx = sem("g_idx")
        g_ones = sem("g_ones")
        g_gx = sem("g_gx")
        g_gacc = sem("g_gacc")
        g_chain = sem("g_chain")
        g_dstT = sem("g_dstT")
        g_eqs = sem("g_eqs")
        g_var = sem("g_var")
        g_std = sem("g_std")
        g_scale = sem("g_scale")
        g_hs = sem("g_hs")
        g_sum = sem("g_sum")
        g_news = sem("g_news")
        g_put = sem("g_put")
        n_in = sem("n_in")
        n_T = sem("n_T")
        n_zTs = sem("n_zTs")
        n_mm = sem("n_mm")
        n_chain = sem("n_chain")
        n_done = sem("n_done")
        n_stored = sem("n_stored")
        sp_gate = sem("sp_gate")
        pool_gate = sem("pool_gate")
        dve_gate = sem("dve_gate")

        def iterations(eng, body):
            body(0, True, False)
            with eng.Fori(1, STEPS // RING - 1) as it:
                body(it, False, False)
            body(STEPS // RING - 1, False, True)

        def edges_broken(eng):
            eng.wait_ge(all_stored, 1)
            eng.wait_ge(flag_ready, 1)
            return eng.value_load(flag_i[0:1, 0:1], min_val=0, max_val=1)

        block = ctx.enter_context(nc.Block())

        @block.sync
        def _(sp):
            sp.dma_start(e_dst[:, :], dst.rearrange("(p e) -> p e", p=SEG_ROWS)).then_inc(dst_loaded, 16)
            sp.wait_ge(next_set, 2)
            with nc.allow_non_contiguous_dma(reason="three numbers per row"):
                sp.dma_start(e_next[0:SEG_ROWS - 1, :],
                             dst.rearrange("(p s e) -> p s e", s=SEGS, e=SEG)[1:SEG_ROWS, 0:3, 0]
                             ).then_inc(next_loaded, 16)
            sp.dma_start(e_src[:, :], src.rearrange("(p e) -> p e", p=SEG_ROWS)).then_inc(src_loaded, 16)
            sp.dma_start(Waug[0:D, 0:D], W).then_inc(w_loaded, 16)
            sp.dma_start(Waug[D:A, 0:D], b.rearrange("(o d) -> o d", o=1)).then_inc(w_loaded, 16)

            def rows(dram, s, half):
                first = s * STEP
                if isinstance(s, int):
                    first = min(first, N - STEP)
                return dram[bass.ds(first + half * (STEP // 2), STEP // 2), :].rearrange(
                    "(w p t) d -> p w (t d)", w=GROUP // 2, t=TILES)

            def load(s, r, half):
                sp.dma_start(x_in[:, r, half * (GROUP // 2):(half + 1) * (GROUP // 2)],
                             rows(x, s, half)).then_inc(x_loaded[r][half], 16)

            def store(s, r, half):
                sp.dma_start(rows(out, s, half), y[:, r, half * (GROUP // 2):(half + 1) * (GROUP // 2)]
                             ).then_inc(stored[r], 16)

            for half in range(2):
                load(0, 0, half)
            for half in range(2):
                load(1, 1, half)

            def body(it, first):
                for r in range(RING):
                    s = it * RING + r
                    for half in range(2):
                        if r > 0 or not first:
                            sp.wait_ge(y_ready, s * 2 - 1 + half)
                        load(s + 2, (r + 2) % RING, half)
                        if r > 0 or not first:
                            store(s - 1, (r - 1) % RING, half)
            body(0, True)
            with sp.Fori(1, STEPS // RING - 1) as it:
                body(it, False)
            for s in range(STEPS - RING, STEPS + 1):
                for half in range(2):
                    sp.wait_ge(y_ready, s * 2 - 1 + half)
                    if s == STEPS and half == 0:
                        sp.wait_ge(stored[(s - 2) % RING], 32 * ((s - 2) // RING + 1))
                    if s + 2 < STEPS:
                        load(s + 2, (s + 2) % RING, half)
                    store(s - 1, (s - 1) % RING, half)
            for r in range(RING):
                sp.wait_ge(stored[r], 32 * (STEPS // RING))
            sp.sem_inc(all_stored, 1)

            with sp.If(edges_broken(sp) != 0):
                sp.dma_start(src_all[:, :], src.rearrange("(p t) -> p t", p=EDGE_ROWS)).then_inc(g_loaded, 16)
                sp.dma_start(dst_all[:, :], dst.rearrange("(p t) -> p t", p=EDGE_ROWS)).then_inc(g_loaded, 16)
                with sp.Fori(0, 100) as i:
                    sp.dma_start(acc_dram[bass.ds(i * 1000, 1000), :].rearrange("(p r) a -> p (r a)", p=125),
                                 zeros[0:125, 0:8 * A]).then_inc(g_cleared, 16)
                sp.dma_start(acc_dram[N:N + P, :], zeros[:, 0:A]).then_inc(g_cleared, 16)
                sp.wait_ge(g_put, 16 * EDGE_TILES)
                with sp.Fori(0, NODE_TILES) as i:
                    sp.dma_start(n_acc[:, :], acc_dram[bass.ds(i * NODE_ROWS, NODE_ROWS), :]).then_inc(n_in, 16)
                    sp.dma_start(n_x[:, :], x[bass.ds(i * NODE_ROWS, NODE_ROWS), :]).then_inc(n_in, 16)
                    sp.wait_ge(n_done, i + 1)
                    sp.dma_start(out[bass.ds(i * NODE_ROWS, NODE_ROWS), :], n_out[:, :]).then_inc(n_stored, 16)
                    sp.wait_ge(n_stored, i * 16 + 16)
                    sp.sem_inc(sp_gate, 1)
                sp.wait_ge(n_stored, 16 * NODE_TILES)
                sp.sem_inc(sp_gate, 1)

        @block.gpsimd
        def _(pool):
            C = 0

            def link(ins):
                nonlocal C
                C += 1
                ins.then_inc(p_chain, 1)

            link(pool.memset(ident[:, :], 0.0))
            link(pool.iota(head_no[:, :], [[SEG, SEGS + 3]], base=0, channel_multiplier=SEGS * SEG,
                           allow_small_or_imprecise_dtypes=True))
            link(pool.iota(rev_pos[:, :], [[-1, SEG]], base=SEG, channel_multiplier=0,
                           allow_small_or_imprecise_dtypes=True))
            link(pool.iota(base[:, :], [[TABLE_ROWS, BLOCKS]], base=0, channel_multiplier=1,
                           allow_small_or_imprecise_dtypes=True))
            pool.wait_ge(p_chain, C)
            pool.affine_select(out=ident[:, :], in_=ident[:, :], compare_op=ALU.not_equal, fill=1.0,
                               base=0, pattern=[[-1, P]], channel_multiplier=1).then_inc(c_pool, 1)
            pool.tensor_scalar(rev_pos[:, :], rev_pos[:, :], float(1 << SRC_BITS), None, ALU.mult).then_inc(c_pool, 1)
            link(pool.tensor_scalar(late[:, :], base[:, :], float(WINDOWS - GROUP), float(-BACK), ALU.is_ge, ALU.mult))
            pool.wait_ge(p_chain, C)
            link(pool.tensor_scalar(base[:, :], base[:, :], float(WINDOW), None, ALU.mult))
            pool.wait_ge(p_chain, C)
            link(pool.tensor_tensor(base[:, :], base[:, :], late[:, :], ALU.add))
            pool.wait_ge(p_chain, C)
            pool.tensor_scalar(base_less[:, :], base[:, :], -0.5, None, ALU.add).then_inc(c_pool, 1)
            pool.wait_ge(dst_loaded, 16)
            pool.tensor_tensor(ahead[:, 0:SEGS * SEG - 1], e_dst[:, 0:SEGS * SEG - 1], e_dst[:, 1:SEGS * SEG],
                               ALU.subtract).then_inc(ahead_ready, 1)
            pool.wait_ge(next_loaded, 16)
            pool.tensor_tensor(ahead[:, SEGS * SEG - 1:], e_dst[:, SEGS * SEG - 1:], e_next[:, 0:1],
                               ALU.subtract).then_inc(ahead_ready, 1)
            pool.iota(own_rows[:, :], [[CAP, SEGS // SPREAD], [0, SPREAD]], base=0,
                      channel_multiplier=LIST_ROWS // 126, allow_small_or_imprecise_dtypes=True).then_inc(c_pool, 1)
            pool.iota(slot_no[:, :], [[1, CAP]], base=-SEG, channel_multiplier=0,
                      allow_small_or_imprecise_dtypes=True).then_inc(c_pool, 1)
            pool.iota(node_no[:, :, :], [[1, TILES], [TILES, P]], base=0, channel_multiplier=0,
                      allow_small_or_imprecise_dtypes=True).then_inc(c_pool, 1)
            pool.iota(node_late[:, :], [[1, LATE * TILES]], base=TILES * SKIP, channel_multiplier=0,
                      allow_small_or_imprecise_dtypes=True).then_inc(c_pool, 1)
            link(pool.memset(later[:, :], 1.0))
            pool.wait_ge(p_chain, C)
            pool.affine_select(out=later[:, :], in_=later[:, :], compare_op=ALU.is_gt, fill=0.0,
                               base=0, pattern=[[1, P]], channel_multiplier=-1).then_inc(c_pool, 1)
            pool.iota(dump_row[:, :], [[0, 1]], base=N, channel_multiplier=1,
                      allow_small_or_imprecise_dtypes=True).then_inc(c_pool, 1)

            pool.wait_ge(heads_ready, 1)
            pool.wait_ge(c_pool, 5)
            link(pool.tensor_tensor(tgt[:, :, :],
                                    heads[:, 0:SEGS].rearrange("p (s o) -> p s o", o=1)
                                    .to_broadcast([SEG_ROWS, SEGS, CAP]),
                                    slot_no.rearrange("p (o c) -> p o c", o=1).to_broadcast([SEG_ROWS, SEGS, CAP]),
                                    ALU.subtract))
            pool.wait_ge(p_chain, C)
            pool.sem_inc(tgt_ready, 1)

            pool.wait_ge(counted, BLOCKS)
            link(pool.tensor_scalar(chunk[:, :], sign_sum[:, :], 0.5, SEG_ROWS * SEGS / 2.0 - 1.0, ALU.mult, ALU.add))
            pool.wait_ge(p_chain, C)
            pool.tensor_scalar(chunk_i[:, :], chunk[:, :], 0.0, None, ALU.max).then_inc(chunk_ready, 1)
            pool.wait_ge(chunk_ready, 1)
            for g in range(BLOCKS):
                pool.indirect_dma_start(out=chunk_dst[:, g, :], out_offset=None,
                                        in_=dst.rearrange("(c e) -> c e", e=SEG),
                                        in_offset=bass.IndirectOffsetOnAxis(ap=chunk_i[:, g:g + 1], axis=0)
                                        ).then_inc(chunk_loaded, 16)
            pool.wait_ge(rank_ready, 1)
            for i in range(SPREAD):
                pool.wait_ge(cleared[i], 16)
            for k, (j0, j1) in enumerate(BATCHES):
                if k < len(BATCHES) - 1:
                    pool.wait_ge(placed, 2 * (k + 1))
                    link(pool.tensor_scalar(valid[:, j0:j1], place[:, j0:j1], 0.5, None, ALU.is_gt))
                    link(pool.tensor_tensor(tgt[:, j0:j1], tgt[:, j0:j1], place[:, j0:j1], ALU.subtract))
                    pool.wait_ge(p_chain, C)
                    link(pool.tensor_tensor(pairs[:, j0:j1, :, 1], tgt[:, j0:j1], valid[:, j0:j1], ALU.mult))
                    pool.wait_ge(p_chain, C)
                else:
                    pool.wait_ge(pairs_ready, 1)
                for j in range(j0, j1):
                    pool.indirect_dma_start(out=packed[j % SPREAD],
                                            out_offset=bass.IndirectOffsetOnAxis(ap=rank_i[:, j:j + 1], axis=0),
                                            in_=pairs[:, j].rearrange("p c k -> p (c k)"),
                                            in_offset=None).then_inc(scattered, 16)
            pool.wait_ge(scattered, 16 * SEGS)
            pool.wait_ge(start_ready, 1)
            for g in range(BLOCKS):
                for i in range(SPREAD):
                    pool.indirect_dma_start(out=wpairs[:, g, i, :], out_offset=None, in_=packed[i],
                                            in_offset=bass.IndirectOffsetOnAxis(ap=start_i[:, g:g + 1], axis=0)
                                            ).then_inc(wpairs_loaded[g], 16)

            def indices(s, r):
                pool.tensor_copy(far_i[:, r, :], src_table[:, bass.ds(s, 1), :].rearrange("p o t -> p (o t)")
                                 ).then_inc(idx_ready, 1)

            pool.wait_ge(table_ready, 1)
            indices(0, 0)

            def body(it, first, last):
                for r in range(RING):
                    s = it * RING + r
                    if r == RING - 1 or not first:
                        pool.wait_ge(gathered[(r + 1) % RING], (it + (r + 1) // RING) * (16 * GS))
                        pool.sem_inc(pool_gate, 1)
                    if first and r == 1:
                        pool.wait_ge(table_ready, BLOCKS)
                    indices(s + 1, (r + 1) % RING)
                    if not first:
                        pool.wait_ge(h_ready, (s - RING + 1) * GROUP)
                        pool.sem_inc(pool_gate, 1)
                    pool.wait_ge(idx_ready, s + 1)
                    pool.sem_inc(pool_gate, 1)
                    for t in range(GS):
                        pool.indirect_dma_start(out=x_far[:, r, t, :], out_offset=None, in_=x,
                                                in_offset=bass.IndirectOffsetOnAxis(ap=far_i[:, r, t:t + 1], axis=0)
                                                ).then_inc(gathered[r], 16)
            iterations(pool, body)

            with pool.If(edges_broken(pool) != 0):
                pool.wait_ge(g_cleared, 16 * 101)
                with pool.Fori(0, EDGE_TILES) as i:
                    pool.wait_ge(g_idx, i + 1)
                    pool.sem_inc(pool_gate, 1)
                    pool.indirect_dma_start(out=g_x[:, :], out_offset=None, in_=x,
                                            in_offset=bass.IndirectOffsetOnAxis(ap=gi_src[:, 0:1], axis=0)
                                            ).then_inc(g_gx, 16)
                    pool.indirect_dma_start(out=g_acc[:, :], out_offset=None, in_=acc_dram,
                                            in_offset=bass.IndirectOffsetOnAxis(ap=gi_dst[:, 0:1], axis=0)
                                            ).then_inc(g_gacc, 16)
                    pool.wait_ge(g_news, i + 1)
                    pool.sem_inc(pool_gate, 1)
                    pool.indirect_dma_start(out=acc_dram,
                                            out_offset=bass.IndirectOffsetOnAxis(ap=gi_put[:, 0:1], axis=0),
                                            in_=g_new[:, :], in_offset=None).then_inc(g_put, 16)
                    pool.wait_ge(g_put, i * 16 + 16)
                    pool.sem_inc(pool_gate, 1)
                pool.wait_ge(g_put, 16 * EDGE_TILES)
                pool.sem_inc(pool_gate, 1)

        @block.vector
        def _(dve):
            C = 0

            def link(ins):
                nonlocal C
                C += 1
                ins.then_inc(d_chain, 1)

            def settle():
                dve.wait_ge(d_chain, C)

            dve.memset(e_next[:, 0:1], float(N)).then_inc(next_set, 1)
            dve.memset(e_next[:, 1:3], float(-10 * N)).then_inc(next_set, 1)
            dve.memset(zeros[:, :], 0.0).then_inc(c_dve, 1)
            link(dve.memset(Waug[:, D:A], 0.0))
            settle()
            dve.memset(Waug[D:A, D:A], 1.0).then_inc(c_dve, 1)
            dve.memset(ones[:, :], 1.0).then_inc(c_dve, 1)
            dve.memset(eps[:, :], EPS).then_inc(c_dve, 1)
            dve.memset(h[:, :, :, D:A], 1.0).then_inc(c_dve, 1)
            dve.memset(faults[:, :], 0.0).then_inc(c_dve, 1)
            link(dve.memset(src_table[:, STEPS:, :], 0))
            link(dve.memset(tgt_table[:, STEPS:, :], 0.0))

            def own_statistics(it, r):
                rows = x_in[:, r].rearrange("p w (t d) -> p d (w t)", d=D)
                for k in range(0, GT, 2):
                    if k * 2 % GT == 0:
                        dve.wait_ge(x_loaded[r][k * 2 // GT], it * 16 + 16)
                    last = dve.bn_stats(stats[:, r, k:k + 2, :].rearrange("p k c -> p (k c)"), rows[:, :, k:k + 2])
                return last

            dve.wait_ge(dst_loaded, 16)
            dve.wait_ge(next_loaded, 16)
            dst_seg = e_dst.rearrange("p (s e) -> p s e", s=SEGS)
            link(dve.tensor_copy(heads[:, SEGS:], e_next[:, :]))
            dve.tensor_copy(heads[:, 0:SEGS], dst_seg[:, :, 0]).then_inc(heads_ready, 1)
            dve.wait_ge(heads_ready, 1)
            dve.wait_ge(c_pool, 2)
            settle()
            link(dve.tensor_tensor(rank[:, :], head_no[:, :], heads[:, :], ALU.subtract))
            dve.wait_ge(src_loaded, 16)
            link(dve.tensor_tensor(far[:, :], e_src[:, :], e_dst[:, :], ALU.not_equal))
            link(dve.tensor_tensor(key[:, :, :], e_src.rearrange("p (s e) -> p s e", s=SEGS),
                                   rev_pos.rearrange("p (o e) -> p o e", o=1).to_broadcast([SEG_ROWS, SEGS, SEG]),
                                   ALU.add))
            dve.wait_ge(ahead_ready, 2)
            settle()
            dve.scalar_tensor_tensor(out=far[:, :], in0=ahead[:, :], scalar=0.0, in1=far[:, :], op0=ALU.is_equal,
                                     op1=ALU.max).then_inc(far_found, 1)
            link(dve.tensor_tensor(gap[:, 0], rank[:, 1:SEGS + 1], rank[:, 0:SEGS], ALU.subtract))
            link(dve.tensor_tensor(gap[:, 1], rank[:, SPREAD:SEGS + SPREAD], rank[:, 0:SEGS], ALU.subtract))
            dve.wait_ge(far_found, 1)
            key_row = key.rearrange("p s e -> p (s e)")
            link(dve.tensor_tensor(key_row, key_row, far[:, :], ALU.mult))
            settle()
            link(dve.tensor_scalar(gap[:, 0], gap[:, 0], float(CAP), None, ALU.is_gt))
            link(dve.tensor_scalar(gap[:, 1], gap[:, 1], float(CAP), None, ALU.is_lt))
            dve.wait_ge(c_dve, 6)
            settle()
            dve.tensor_reduce(faults[0:SEG_ROWS, 1:3], gap[:, :, :], AX.X, ALU.add).then_inc(tests_ready, 1)

            def pick(j0, j1):
                replaced = {}
                for k in range(ROUNDS):
                    taken = {}
                    for j in range(j0, j1):
                        if k > 0:
                            dve.wait_ge(d_chain, replaced[j])
                        link(dve.max(found[:, j, 8 * k:8 * k + 8], key[:, j, :]))
                        taken[j] = C
                    if k < ROUNDS - 1:
                        for j in range(j0, j1):
                            dve.wait_ge(d_chain, taken[j])
                            link(dve.match_replace(out=key[:, j, :], in_to_replace=found[:, j, 8 * k:8 * k + 8],
                                                   in_values=key[:, j, :], imm_value=0.0))
                            replaced[j] = C

            def split(j0, j1):
                settle()
                link(dve.tensor_copy(found_i[:, j0:j1], found[:, j0:j1]))
                settle()
                link(dve.tensor_scalar(part_i[:, 0, j0:j1], found_i[:, j0:j1], (1 << SRC_BITS) - 1, None,
                                       ALU.bitwise_and))
                link(dve.tensor_scalar(part_i[:, 1, j0:j1], found_i[:, j0:j1], SRC_BITS, None,
                                       ALU.arith_shift_right))
                settle()
                dve.sem_inc(picked, 1)

            pick(*BATCHES[0])
            split(*BATCHES[0])
            dve.wait_ge(tests_summed, 1)
            dve.wait_ge(c_pool, 5)
            link(dve.tensor_reduce(fine[:, 0:1], ps[0:SEG_ROWS, 3, 0:3], AX.X, ALU.add))
            link(dve.tensor_scalar(fine[:, 1:2], ps[0:SEG_ROWS, 3, 9:10], float(FAR), None, ALU.is_equal))
            link(dve.tensor_tensor(rank[:, 0:SEGS], rank[:, 0:SEGS], own_rows[:, :], ALU.subtract))
            settle()
            link(dve.scalar_tensor_tensor(out=fine[:, 2:3], in0=fine[:, 0:1], scalar=0.0, in1=fine[:, 1:2],
                                          op0=ALU.is_equal, op1=ALU.mult))
            settle()
            dve.scalar_tensor_tensor(out=rank_i[:, :], in0=rank[:, 0:SEGS], scalar=fine[:, 2:3], in1=own_rows[:, :],
                                     op0=ALU.mult, op1=ALU.add).then_inc(rank_ready, 1)
            for k in range(1, len(BATCHES)):
                pick(*BATCHES[k])
                split(*BATCHES[k])
            J = slice(*BATCHES[-1])
            dve.wait_ge(tgt_ready, 1)
            link(dve.tensor_scalar(valid[:, J], part_i[:, 1, J], 0.5, None, ALU.is_gt))
            link(dve.tensor_tensor(tgt[:, J], tgt[:, J], part_i[:, 1, J], ALU.subtract))
            settle()
            dve.wait_ge(placed, 2 * len(BATCHES))
            dve.tensor_tensor(pairs[:, J, :, 1], tgt[:, J], valid[:, J], ALU.mult).then_inc(pairs_ready, 1)

            dve.wait_ge(chunk_ready, 1)
            dve.wait_ge(chunk_loaded, 16 * BLOCKS)
            for g in range(BLOCKS):
                link(dve.tensor_scalar(below_c[:, g, :], chunk_dst[:, g, :], base[:, g:g + 1], None, ALU.is_lt))
            settle()
            link(dve.tensor_reduce(start[:, :], below_c[:, :, :], AX.X, ALU.add))
            settle()
            link(dve.scalar_tensor_tensor(out=start[:, :], in0=chunk_i[:, :], scalar=float(SEG), in1=start[:, :],
                                          op0=ALU.mult, op1=ALU.add))
            settle()
            link(dve.tensor_tensor(start[:, :], start[:, :], base[:, :], ALU.subtract))
            settle()
            link(dve.tensor_scalar(start[:, :], start[:, :], 0.0, float(FAR), ALU.max, ALU.min))
            settle()
            dve.tensor_copy(start_i[:, :], start[:, :]).then_inc(start_ready, 1)
            own_statistics(0, 0)

            for g in range(BLOCKS):
                dve.wait_ge(wpairs_loaded[g], 16 * SPREAD)
                link(dve.tensor_tensor(wpairs[:, g, 0], wpairs[:, g, 0], wpairs[:, g, 1], ALU.add))
                settle()
                link(dve.tensor_tensor(wpairs[:, g, 0], wpairs[:, g, 0], wpairs[:, g, 2], ALU.add))
                settle()
                got = wpairs[:, g, 0].rearrange("p (c k) -> p k c", k=2)
                link(dve.tensor_scalar(wedge[:, g, 0, :], got[:, 0, :], 0.0, float(N - 1), ALU.max, ALU.min))
                link(dve.tensor_scalar(wedge[:, g, 1, :], got[:, 1, :], base[:, g:g + 1], None, ALU.subtract))
                settle()
                dve.sem_inc(wedge_ready, 1)
                link(dve.tensor_scalar(wtest[:, g, 0:1], start[:, g:g + 1], float(FAR - PACKED), None, ALU.is_lt))
                link(dve.tensor_scalar(wtest[:, g, 1:2], start[:, g:g + 1], float(FAR - P), None, ALU.is_lt))
                settle()
                link(dve.scalar_tensor_tensor(out=faults[0:TABLE_ROWS, 3 + 2 * g:4 + 2 * g],
                                              in0=wedge[:, g, 1, PACKED:PACKED + 1], scalar=float(WINDOW),
                                              in1=wtest[:, g, 0:1], op0=ALU.is_lt, op1=ALU.mult))
                link(dve.scalar_tensor_tensor(out=faults[0:TABLE_ROWS, 4 + 2 * g:5 + 2 * g],
                                              in0=wedge[:, g, 1, P:P + 1], scalar=float(TILES * SKIP),
                                              in1=wtest[:, g, 1:2], op0=ALU.is_lt, op1=ALU.mult))
                dve.wait_ge(turned, 2 * SLOTS * (g + 1))
                for kind, table in enumerate((src_table, tgt_table)):
                    for t in range(SLOTS):
                        link(dve.tensor_copy(
                            table[:, g * BLOCK_STEPS:(g + 1) * BLOCK_STEPS, :]
                            .rearrange("p s (w t) -> p s w t", t=SLOTS)[:, :, :, t],
                            ps[:, 4 + kind * SLOTS + t, 0:TABLE_ROWS].rearrange("p (s w) -> p s w", w=GROUP)))
                settle()
                dve.sem_inc(table_ready, 1)
            link(dve.tensor_reduce(flag[:, 0:1], faults[:, 0:9], AX.X, ALU.add))
            settle()
            link(dve.tensor_copy(flag[:, 1:2], faults[:, 9:10]))
            settle()
            dve.sem_inc(faults_ready, 1)
            dve.wait_ge(faults_summed, 1)
            link(dve.tensor_scalar(flag[0:1, 2:3], ps[0:1, 0, 1:2], float(FAR), None, ALU.not_equal))
            settle()
            link(dve.tensor_tensor(flag[0:1, 3:4], ps[0:1, 0, 0:1], flag[0:1, 2:3], ALU.add))
            settle()
            dve.tensor_scalar(flag_i[:, :], flag[0:1, 3:4], 1.0, None, ALU.min).then_inc(flag_ready, 1)

            dve.wait_ge(c_pool, 7)

            def far_statistics(it, r):
                dve.wait_ge(gathered[r], it * (16 * GS) + 16 * GS)
                rows = x_far[:, r].rearrange("p k d -> p d k")
                for k in range(0, GS, 2):
                    last = dve.bn_stats(stats[:, r, GT + k:GT + k + 2, :].rearrange("p k c -> p (k c)"),
                                        rows[:, :, k:k + 2])
                return last

            def targets(it, r):
                dve.tensor_copy(far_n[:, r, :], tgt_table[:, bass.ds(it * RING + r, 1), :].rearrange("p o t -> p (o t)")
                                ).then_inc(far_ready, 1)

            def hits(it, r, w):
                s = it * RING + r
                if w == 0:
                    if not (isinstance(s, int) and s < RING):
                        dve.wait_ge(z_ready, (s - RING + 1) * GROUP)
                    dve.wait_ge(far_ready, s + 1)
                early_hits(r, w)
                late_hits(r, w)

            def early_hits(r, w):
                dve.tensor_scalar(hit0[:, r, w], node_no[:, :, :], far_n[:, r, SLOTS * w:SLOTS * w + 1], None,
                                  ALU.is_equal)

            def late_hits(r, w):
                dve.tensor_scalar(hit1[:, r, w], node_late[:, :], far_n[:, r, SLOTS * w + 1:SLOTS * w + 2],
                                  None, ALU.is_equal).then_inc(hits_ready, 1)

            def inverse(it, r):
                dve.wait_ge(std_ready, it * RING + r + 1)
                dve.reciprocal(ln[:, r, 1], ln[:, r, 0]).then_inc(ln_chain, 1)

            def shift(it, r):
                dve.wait_ge(stats_ready, it * RING + r + 1)
                dve.wait_ge(ln_chain, it * RING + r + 1)
                dve.scalar_tensor_tensor(out=ln[:, r, 2], in0=stats[:, r, :, 1], scalar=-1.0, in1=ln[:, r, 1],
                                         op0=ALU.mult, op1=ALU.mult).then_inc(ln_ready, 1)

            def copy_zT(it, r, first):
                s = it * RING + r
                dve.wait_ge(z_ready, s * GROUP + DVE_COPY + 1)
                if not first:
                    dve.wait_ge(m_ready, (s - 1) * GROUP + DVE_COPY + 1)
                dve.tensor_copy(zT[:, DVE_COPY, :], ps[0:A, DVE_COPY, 0:WINDOW]).then_inc(zT_copied, 1)

            def half_of(it, r, half):
                s = it * RING + r
                w0 = half * (GROUP // 2)
                M = ps[:, 4 + w0:4 + w0 + GROUP // 2, 0:TILES * A].rearrange("p w (t a) -> p w t a", t=TILES)
                return s, w0, M

            def degrees(it, r, half):
                s, w0, M = half_of(it, r, half)
                dve.wait_ge(m_ready, s * GROUP + w0 + GROUP // 2)
                dve.reciprocal(recip[:, half], M[:, :, :, D]).then_inc(f_chain, 1)

            def divide(it, r, half):
                s, w0, M = half_of(it, r, half)
                dve.wait_ge(f_chain, s * 2 + half + 1)
                dve.tensor_tensor(scaled[:, half], M[:, :, :, 0:D],
                                  recip[:, half].rearrange("p w (t o) -> p w t o", o=1)
                                  .to_broadcast([P, GROUP // 2, TILES, D]), ALU.mult).then_inc(f_read, 1)

            def add_x(it, r, half):
                s, w0, M = half_of(it, r, half)
                if half == 0 and not (isinstance(s, int) and s < RING):
                    dve.wait_ge(stored[r], it * 32)
                dve.wait_ge(f_read, s * 2 + half + 1)
                dve.tensor_tensor(y[:, r, w0:w0 + GROUP // 2],
                                  scaled[:, half].rearrange("p w t d -> p w (t d)"),
                                  x_in[:, r, w0:w0 + GROUP // 2], ALU.add).then_inc(y_ready, 1)

            dve.wait_ge(table_ready, BLOCKS)
            targets(0, 0)
            far_statistics(0, 0).then_inc(stats_ready, 1)
            for w in range(GROUP - 1):
                hits(0, 0, w)
            early_hits(0, GROUP - 1)
            late_hits(0, GROUP - 1)
            inverse(0, 0)
            shift(0, 0)

            def body(it, first, last):
                for r in range(RING):
                    before = (it, r - 1) if r > 0 else (it - 1, RING - 1)
                    after = (it, r + 1) if r < RING - 1 else (it + 1, 0)
                    old = r > 0 or not first
                    new = r < RING - 1 or not last
                    if new:
                        targets(*after)
                        own_statistics(*after)
                        far_statistics(*after).then_inc(stats_ready, 1)
                    if old:
                        degrees(*before, 1)
                    if new:
                        hits(*after, 0)
                    if old:
                        divide(*before, 1)
                    copy_zT(it, r, first and r == 0)
                    if new:
                        hits(*after, 1)
                    if old:
                        add_x(*before, 1)
                    if new:
                        inverse(*after)
                        early_hits(after[1], 2)
                        shift(*after)
                        late_hits(after[1], 2)
                    degrees(it, r, 0)
                    if new:
                        early_hits(after[1], 3)
                    divide(it, r, 0)
                    if new:
                        late_hits(after[1], 3)
                    add_x(it, r, 0)

            iterations(dve, body)
            degrees(STEPS // RING - 1, RING - 1, 1)
            divide(STEPS // RING - 1, RING - 1, 1)
            add_x(STEPS // RING - 1, RING - 1, 1)

            with dve.If(edges_broken(dve) != 0):
                dve.memset(g_h[:, D:A], 1.0).then_inc(g_ones, 1)
                dve.wait_ge(g_loaded, 32)
                with dve.Fori(0, EDGE_TILES) as i:
                    c = i * 9
                    dve.tensor_copy(gi_src[:, :], src_all[:, bass.ds(i, 1)]).then_inc(g_chain, 1)
                    dve.tensor_copy(gi_dst[:, :], dst_all[:, bass.ds(i, 1)]).then_inc(g_chain, 1)
                    dve.tensor_copy(g_dst[:, :], dst_all[:, bass.ds(i, 1)]).then_inc(g_chain, 1)
                    dve.wait_ge(g_chain, c + 3)
                    dve.tensor_copy(g_dstb[:, :], g_dst[:, 0:1].to_broadcast([EDGE_ROWS, EDGE_ROWS])).then_inc(g_idx, 1)
                    dve.wait_ge(g_dstT, i + 1)
                    dve.tensor_scalar(g_eq[:, :], ps[0:EDGE_ROWS, 0, 0:EDGE_ROWS], g_dst[:, 0:1], None,
                                      ALU.is_equal).then_inc(g_eqs, 1)
                    dve.wait_ge(g_eqs, i + 1)
                    dve.tensor_tensor_reduce(out=g_eql[:, :], in0=g_eq[:, :], in1=later[0:EDGE_ROWS, 0:EDGE_ROWS],
                                             scale=1.0, scalar=0.0, op0=ALU.mult, op1=ALU.add,
                                             accum_out=g_small[:, 8:9]).then_inc(g_chain, 1)
                    dve.wait_ge(g_chain, c + 4)
                    dve.tensor_scalar(g_small[:, 9:10], g_small[:, 8:9], 1.0, None, ALU.min).then_inc(g_chain, 1)
                    dve.tensor_tensor(g_small[:, 10:11], dump_row[0:EDGE_ROWS, :], g_dst[:, 0:1],
                                      ALU.subtract).then_inc(g_chain, 1)
                    dve.wait_ge(g_chain, c + 6)
                    dve.scalar_tensor_tensor(out=gi_put[:, :], in0=g_small[:, 10:11], scalar=g_small[:, 9:10],
                                             in1=g_dst[:, :], op0=ALU.mult, op1=ALU.add).then_inc(g_chain, 1)
                    dve.wait_ge(g_gx, i * 16 + 16)
                    dve.bn_stats(g_small[:, 0:6], g_x[:, :]).then_inc(g_chain, 1)
                    dve.wait_ge(g_chain, c + 8)
                    dve.sem_inc(dve_gate, 1)
                    dve.bn_aggr(g_small[:, 11:13], g_small[:, 0:6]).then_inc(g_chain, 1)
                    dve.wait_ge(g_chain, c + 9)
                    dve.tensor_scalar(g_small[:, 13:14], g_small[:, 12:13], EPS, None, ALU.add).then_inc(g_var, 1)
                    dve.wait_ge(g_std, i + 1)
                    dve.reciprocal(g_small[:, 15:16], g_small[:, 14:15]).then_inc(g_scale, 1)
                    dve.wait_ge(g_scale, i * 2 + 1)
                    dve.scalar_tensor_tensor(out=g_small[:, 8:9], in0=g_small[:, 11:12], scalar=-1.0,
                                             in1=g_small[:, 15:16], op0=ALU.mult, op1=ALU.mult).then_inc(g_scale, 1)
                    dve.wait_ge(g_sum, i + 1)
                    dve.wait_ge(g_gacc, i * 16 + 16)
                    dve.tensor_tensor(g_new[:, :], ps[0:EDGE_ROWS, 1, 0:A], g_acc[:, :], ALU.add).then_inc(g_news, 1)
                    dve.wait_ge(g_put, i * 16 + 16)
                    dve.sem_inc(dve_gate, 1)
                with dve.Fori(0, NODE_TILES) as i:
                    dve.wait_ge(n_T, i + 1)
                    dve.tensor_copy(n_zT[:, :], ps[0:A, 2, 0:NODE_ROWS]).then_inc(n_zTs, 1)
                    dve.wait_ge(n_mm, i + 1)
                    dve.tensor_scalar(n_deg[:, 0:1], ps[0:NODE_ROWS, 3, D:A], 1.0, None, ALU.max).then_inc(n_chain, 1)
                    dve.wait_ge(n_chain, i * 2 + 1)
                    dve.reciprocal(n_deg[:, 1:2], n_deg[:, 0:1]).then_inc(n_chain, 1)
                    dve.wait_ge(n_chain, i * 2 + 2)
                    dve.scalar_tensor_tensor(out=n_out[:, :], in0=ps[0:NODE_ROWS, 3, 0:D], scalar=n_deg[:, 1:2],
                                             in1=n_x[:, :], op0=ALU.mult, op1=ALU.add).then_inc(n_done, 1)

        @block.scalar
        def _(act):
            act.wait_ge(c_dve, 1)
            for i in range(SPREAD):
                act.dma_start(packed[i].rearrange("(p r) k -> p (r k)", p=126),
                              zeros[0:126, :]).then_inc(cleared[i], 16)
            act.wait_ge(heads_spread, SEGS)
            act.wait_ge(c_pool, 3)
            for g in range(BLOCKS):
                act.activation(signs[:, g].rearrange("p (k n) -> p k n", k=SPREAD),
                               ps[0:TABLE_ROWS, 0:SPREAD, 0:SEG_ROWS * BANK_SEGS], ACT.Sign,
                               bias=base_less[:, g:g + 1], scale=-1.0,
                               accum_out=sign_sum[:, g:g + 1]).then_inc(counted, 1)
            act.wait_ge(c_dve, 6)
            act.wait_ge(ahead_ready, 2)
            act.activation(spare[:, 0], ahead[:, :], ACT.Relu, accum_out=faults[0:SEG_ROWS, 0:1]).then_inc(summed, 1)
            act.wait_ge(far_found, 1)
            act.activation(spare[:, 1], far[:, :], ACT.Copy, accum_out=faults[0:SEG_ROWS, 9:10]).then_inc(summed, 1)

            for k, (j0, j1) in enumerate(BATCHES):
                act.wait_ge(picked, k + 1)
                act.activation(pairs[:, j0:j1, :, 0], part_i[:, 0, j0:j1], ACT.Copy).then_inc(placed, 1)
                act.activation(place[:, j0:j1], part_i[:, 1, j0:j1], ACT.Copy).then_inc(placed, 1)

            def copy_zT(s, w, first):
                if w == DVE_COPY:
                    return
                act.wait_ge(z_ready, s * GROUP + w + 1)
                if not first:
                    act.wait_ge(m_ready, (s - 1) * GROUP + w + 1)
                act.activation(zT[:, w, :], ps[0:A, w, 0:WINDOW], ACT.Copy).then_inc(zT_ready, 1)

            def deviation(s, r):
                act.wait_ge(stats_ready, s + 1)
                act.activation(ln[:, r, 0], stats[:, r, :, 2], ACT.Sqrt, bias=eps[:, :],
                               scale=1.0 / D).then_inc(std_ready, 1)

            deviation(0, 0)

            def body(it, first, last):
                for r in range(RING):
                    s = it * RING + r
                    L = ln[:, r]
                    if not first:
                        act.wait_ge(z_ready, (s - RING + 1) * GROUP)
                    act.wait_ge(ln_ready, s + 1)
                    for w in range(GROUP):
                        for t in range(SLOTS):
                            k = GT + w * SLOTS + t
                            act.activation(h[:, r, k, 0:D], x_far[:, r, w * SLOTS + t, :], ACT.Relu,
                                           bias=L[:, 2, k:k + 1], scale=L[:, 1, k:k + 1])
                        if w == 2 and not (last and r == RING - 1):
                            deviation(s + 1, (r + 1) % RING)
                        for t in range(TILES):
                            k = w * TILES + t
                            done = act.activation(h[:, r, k, 0:D], x_in[:, r, w, t * D:t * D + D], ACT.Relu,
                                                  bias=L[:, 2, k:k + 1], scale=L[:, 1, k:k + 1])
                        done.then_inc(h_ready, 1)
                        if w > 0:
                            copy_zT(s, w - 1, first and r == 0)
                        elif r > 0 or not first:
                            copy_zT(s - 1, GROUP - 1, first and r == 1)
            iterations(act, body)
            copy_zT(STEPS - 1, GROUP - 1, False)

            with act.If(edges_broken(act) != 0):
                with act.Fori(0, EDGE_TILES) as i:
                    act.wait_ge(g_var, i + 1)
                    act.activation(g_small[:, 14:15], g_small[:, 13:14], ACT.Sqrt).then_inc(g_std, 1)
                    act.wait_ge(g_scale, i * 2 + 2)
                    act.activation(g_h[:, 0:D], g_x[:, :], ACT.Relu, bias=g_small[:, 8:9],
                                   scale=g_small[:, 15:16]).then_inc(g_hs, 1)

        @block.tensor
        def _(pe):
            pe.wait_ge(c_dve, 6)
            pe.wait_ge(c_pool, 1)
            pe.wait_ge(heads_ready, 1)
            for j in range(SEGS):
                pe.matmul(ps[0:TABLE_ROWS, j // BANK_SEGS,
                             (j % BANK_SEGS) * SEG_ROWS:(j % BANK_SEGS + 1) * SEG_ROWS],
                          heads[:, j:j + 1].to_broadcast([SEG_ROWS, TABLE_ROWS]), ident[0:SEG_ROWS, 0:SEG_ROWS],
                          start=True, stop=True).then_inc(heads_spread, 1)
            pe.wait_ge(tests_ready, 1)
            pe.wait_ge(summed, 2)
            pe.matmul(ps[0:SEG_ROWS, 3, 0:10], ones[0:SEG_ROWS, 0:SEG_ROWS], faults[0:SEG_ROWS, :],
                      start=True, stop=True).then_inc(tests_summed, 1)
            pe.wait_ge(w_loaded, 32)
            pe.wait_ge(c_pool, 9)
            for g in range(BLOCKS):
                pe.wait_ge(wedge_ready, g + 1)
                if g > 0:
                    pe.wait_ge(table_ready, g)
                for kind in range(2):
                    for t in range(SLOTS):
                        pe.transpose(ps[:, 4 + kind * SLOTS + t, 0:TABLE_ROWS], wedge[:, g, kind, t * P:(t + 1) * P],
                                     ident[0:TABLE_ROWS, 0:TABLE_ROWS]).then_inc(turned, 1)
            pe.wait_ge(faults_ready, 1)
            pe.matmul(ps[0:1, 0, 0:2], ones[:, 0:1], flag[:, 0:2], start=True, stop=True).then_inc(faults_summed, 1)
            pe.wait_ge(flag_ready, 1)

            def zT_taken(s, w):
                if w == DVE_COPY:
                    pe.wait_ge(zT_copied, s + 1)
                else:
                    pe.wait_ge(zT_ready, s * (GROUP - 1) + w + (w < DVE_COPY))

            def sums(s, r, w, first):
                pe.wait_ge(h_ready, s * GROUP + w + 1)
                pe.wait_ge(hits_ready, s * GROUP + w + 1)
                if not first:
                    zT_taken(s - 1, w)
                for t in range(TILES):
                    pe.matmul(ps[0:A, w, t * P:(t + 1) * P], h[:, r, w * TILES + t, :], ident[:, :],
                              start=(t == 0), stop=False, is_transpose=True)
                pe.matmul(ps[0:A, w, 0:WINDOW], h[:, r, GT + w * SLOTS, :], hit0[:, r, w].rearrange("p t n -> p (t n)"),
                          start=False, stop=False)
                pe.matmul(ps[0:A, w, 0:WINDOW].rearrange("p (t n) -> p t n", t=TILES)[:, :, SKIP:],
                          h[:, r, GT + w * SLOTS + 1, :], hit1[:, r, w].rearrange("p (n t) -> p t n", t=TILES),
                          start=False, stop=True).then_inc(z_ready, 1)

            def product(s, w, first):
                zT_taken(s, w)
                if not first:
                    pe.wait_ge(f_read, (s - 1) * 2 + w // 2 + 1)
                for t in range(TILES):
                    last = pe.matmul(ps[:, 4 + w, t * A:(t + 1) * A], zT[:, w, t * P:(t + 1) * P], Waug[:, :],
                                     start=True, stop=True)
                last.then_inc(m_ready, 1)

            def body(it, first, last):
                for r in range(RING):
                    s = it * RING + r
                    for w in range(GROUP):
                        sums(s, r, w, first and r == 0)
                        if w > 0:
                            product(s, w - 1, first and r == 0)
                        elif r > 0 or not first:
                            product(s - 1, GROUP - 1, first and r == 1)
            iterations(pe, body)
            product(STEPS - 1, GROUP - 1, False)

            with pe.If(edges_broken(pe) != 0):
                pe.wait_ge(g_ones, 1)
                with pe.Fori(0, EDGE_TILES) as i:
                    pe.wait_ge(g_idx, i + 1)
                    pe.transpose(ps[0:EDGE_ROWS, 0, 0:EDGE_ROWS], g_dstb[:, :],
                                 ident[0:EDGE_ROWS, 0:EDGE_ROWS]).then_inc(g_dstT, 1)
                    pe.wait_ge(g_eqs, i + 1)
                    pe.wait_ge(g_hs, i + 1)
                    pe.matmul(ps[0:EDGE_ROWS, 1, 0:A], g_eq[:, :], g_h[:, :], start=True, stop=True).then_inc(g_sum, 1)
                with pe.Fori(0, NODE_TILES) as i:
                    pe.wait_ge(n_in, i * 32 + 32)
                    pe.transpose(ps[0:A, 2, 0:NODE_ROWS], n_acc[:, :],
                                 ident[0:NODE_ROWS, 0:NODE_ROWS]).then_inc(n_T, 1)
                    pe.wait_ge(n_zTs, i + 1)
                    pe.matmul(ps[0:NODE_ROWS, 3, 0:A], n_zT[:, :], Waug[:, :], start=True, stop=True).then_inc(n_mm, 1)


_INS = ["x", "src", "dst", "L0_gnn_W", "L0_gnn_b"]


def kernel(**inputs):
    import numpy as _np
    import concourse.bacc as _bacc
    from concourse import mybir as _mybir
    from concourse.bass_utils import run_bass_kernel_spmd as _run

    nc = _bacc.Bacc("TRN2", target_bir_lowering=False, num_devices=1)
    arrays, args = {}, []
    for name in _INS:
        a = _np.ascontiguousarray(inputs[name])
        arrays[f"in_{name}_dram"] = a
        args.append(nc.dram_tensor(f"in_{name}_dram", a.shape, _mybir.dt.from_np(a.dtype), kind="ExternalInput").ap())
    args.append(nc.dram_tensor("out_0_dram", inputs["x"].shape, _mybir.dt.float32, kind="ExternalOutput").ap())
    gnn_layer(nc, *args)
    r = _run(nc, [arrays], core_ids=[0])
    return r.results[0]["out_0_dram"]
```
